# Optimizing a Trainium2 kernel written in Bass

```python
import numpy as np
import jax
import jax.numpy as jnp

def _softmax(x, axis=-1):
    return jax.nn.softmax(x, axis=axis)

def _gelu(x):
    return jax.nn.gelu(x, approximate=True)

def _silu(x):
    return jax.nn.silu(x)

def _sigmoid(x):
    return jax.nn.sigmoid(x)

def _layernorm(x, axis=-1, eps=1e-05):
    m = jnp.mean(x, axis=axis, keepdims=True)
    v = jnp.var(x, axis=axis, keepdims=True)
    return (x - m) / jnp.sqrt(v + eps)

def _scatter_add(tgt, idx, src, axis=0):
    return tgt.at[idx].add(src)

def _segment_sum(src, seg, n):
    return jax.ops.segment_sum(src, seg, n)
kernel_name = 'mk_seq_postln_d1_jaxref_r8_15ba76'

def setup_inputs(seed: int=0):
    np.random.seed(seed)
    _w = jnp.asarray

    def _L0_attn_setup():
        import jax, jax.numpy as jnp
        import numpy as np
        D_MODEL = 256
        N_HEADS = 16
        SEQ_LEN = 256
        BATCH = 2
        BIAS_MAX = 8.0

        def alibi_bias(n_heads, seq_len, dtype):
            pos = jnp.arange(1 - seq_len, 1, dtype=dtype)
            m = jnp.arange(1, n_heads + 1, dtype=dtype) * (BIAS_MAX / n_heads)
            slopes = 1.0 / 2.0 ** m
            return pos[None, :] * slopes[:, None]
        key = jax.random.key(seed)
        k1, k2, k3 = jax.random.split(key, 3)
        s = 1.0 / np.sqrt(D_MODEL)
        x = jax.random.normal(k1, (BATCH, SEQ_LEN, D_MODEL), dtype=jnp.float32)
        Wqkv = jax.random.normal(k2, (3 * D_MODEL, D_MODEL), dtype=jnp.float32) * s
        b_qkv = jnp.zeros((3 * D_MODEL,), dtype=jnp.float32)
        Wout = jax.random.normal(k3, (D_MODEL, D_MODEL), dtype=jnp.float32) * s
        b_out = jnp.zeros((D_MODEL,), dtype=jnp.float32)
        return {'x': x, 'Wqkv': Wqkv, 'b_qkv': b_qkv, 'Wout': Wout, 'b_out': b_out}
    _L0_attn_in = _L0_attn_setup()

    def _L0_ffn_setup():
        import jax, jax.numpy as jnp
        import numpy as np
        TOP_K = 8
        key = jax.random.key(seed)
        k0, k1, k2, k3, k4 = jax.random.split(key, 5)
        B, S, H = (1, 128, 256)
        E, I = (64, 96)
        return {'hidden_states': jax.random.normal(k0, (B, S, H), dtype=jnp.float32), 'gate_w': jax.random.normal(k1, (E, H), dtype=jnp.float32) * 0.02, 'w1': jax.random.normal(k2, (E, H, I), dtype=jnp.float32) * 0.02, 'w3': jax.random.normal(k3, (E, H, I), dtype=jnp.float32) * 0.02, 'w2': jax.random.normal(k4, (E, I, H), dtype=jnp.float32) * 0.02}
    _L0_ffn_in = _L0_ffn_setup()
    _d = {'L0_attn_x': _L0_attn_in['x'], 'L0_attn_Wqkv': _L0_attn_in['Wqkv'], 'L0_attn_b_qkv': _L0_attn_in['b_qkv'], 'L0_attn_Wout': _L0_attn_in['Wout'], 'L0_attn_b_out': _L0_attn_in['b_out'], 'L0_ffn_gate_w': _L0_ffn_in['gate_w'], 'L0_ffn_w1': _L0_ffn_in['w1'], 'L0_ffn_w3': _L0_ffn_in['w3'], 'L0_ffn_w2': _L0_ffn_in['w2']}
    _x0 = _d['L0_attn_x']
    _d['L0_attn_x'] = jax.random.normal(jax.random.fold_in(jax.random.key(seed), 1), (2, 512, 256), dtype=_x0.dtype)
    del _x0
    return _d

def reference(L0_attn_x, L0_attn_Wqkv, L0_attn_b_qkv, L0_attn_Wout, L0_attn_b_out, L0_ffn_gate_w, L0_ffn_w1, L0_ffn_w3, L0_ffn_w2):

    def _L0_attn_ref(x, Wqkv, b_qkv, Wout, b_out):
        import jax, jax.numpy as jnp
        import numpy as np
        D_MODEL = 256
        N_HEADS = 16
        SEQ_LEN = 256
        BATCH = 2
        BIAS_MAX = 8.0

        def alibi_bias(n_heads, seq_len, dtype):
            pos = jnp.arange(1 - seq_len, 1, dtype=dtype)
            m = jnp.arange(1, n_heads + 1, dtype=dtype) * (BIAS_MAX / n_heads)
            slopes = 1.0 / 2.0 ** m
            return pos[None, :] * slopes[:, None]
        B, S, D = x.shape
        H = N_HEADS
        hd = D // H
        scale = 1.0 / jnp.sqrt(jnp.asarray(hd, dtype=x.dtype))
        qkv = x @ Wqkv.T + b_qkv
        q, k, v = jnp.split(qkv, 3, axis=-1)
        q = q.reshape(B, S, H, hd)
        k = k.reshape(B, S, H, hd)
        v = v.reshape(B, S, H, hd)
        scores = jnp.einsum('bqhd,bkhd->bhqk', q, k) * scale
        bias = alibi_bias(H, S, x.dtype)
        scores = scores + bias[None, :, None, :]
        causal = jnp.tril(jnp.ones((S, S), dtype=bool))
        scores = jnp.where(causal[None, None, :, :], scores, jnp.asarray(-1000000000.0, dtype=x.dtype))
        p = jax.nn.softmax(scores, axis=-1)
        ctx = jnp.einsum('bhqk,bkhd->bqhd', p, v).reshape(B, S, D)
        return ctx @ Wout.T + b_out

    def _L0_ffn_ref(hidden_states, gate_w, w1, w3, w2):
        import jax, jax.numpy as jnp
        import numpy as np
        TOP_K = 8
        B, S, H = hidden_states.shape
        x = hidden_states.reshape(-1, H)
        T = x.shape[0]
        E = gate_w.shape[0]
        logits = x.astype(jnp.float32) @ gate_w.T
        probs = jax.nn.softmax(logits, axis=-1)
        topk_w, topk_idx = jax.lax.top_k(probs, TOP_K)
        topk_w = topk_w / (jnp.sum(topk_w, axis=-1, keepdims=True) + 1e-20)
        combine_w = jnp.zeros((T, E), dtype=probs.dtype).at[jnp.arange(T)[:, None], topk_idx].add(topk_w)
        g = jnp.einsum('th,ehi->tei', x, w1)
        u = jnp.einsum('th,ehi->tei', x, w3)
        a = jax.nn.silu(g) * u
        y = jnp.einsum('te,tei,eih->th', combine_w.astype(x.dtype), a, w2)
        return y.reshape(B, S, H)
    x = L0_attn_x
    x = _layernorm(x + _L0_attn_ref(x, L0_attn_Wqkv, L0_attn_b_qkv, L0_attn_Wout, L0_attn_b_out), axis=-1)
    x = _layernorm(x + _L0_ffn_ref(x, L0_ffn_gate_w, L0_ffn_w1, L0_ffn_w3, L0_ffn_w2), axis=-1)
    return x

_drawn_inputs = setup_inputs


def setup_inputs(seed=0):
    import zlib

    import numpy as np

    out = dict(_drawn_inputs(seed))
    spreads = {'L0_attn_b_qkv': (0.0, 0.1), 'L0_attn_b_out': (0.0, 0.1)}
    factors = {'L0_ffn_gate_w': 8.0, 'L0_ffn_w1': 8.0, 'L0_ffn_w3': 8.0, 'L0_ffn_w2': 8.0}
    for name, (base, spread) in spreads.items():
        noise = np.random.default_rng([zlib.crc32(name.encode()), seed]).standard_normal(out[name].shape)
        drawn = base * np.exp(spread * noise) if base else spread * noise
        out[name] = jnp.asarray(drawn.astype(out[name].dtype))
    for name, factor in factors.items():
        out[name] = (out[name] * factor).astype(out[name].dtype)
    return out
```

```python
from contextlib import ExitStack

import numpy as np

import concourse.bass as bass
from concourse import mybir

F32 = mybir.dt.float32
BF16 = mybir.dt.bfloat16
F16 = mybir.dt.float16
I32 = mybir.dt.int32
U32 = mybir.dt.uint32
ALU = mybir.AluOpType
ACT = mybir.ActivationFunctionType
AX = mybir.AxisListType

P = 128
NEG = -1.0e30
SLOTS = 3
PRING = 4


def alibi_rows(heads, seq):
    pos = np.arange(1 - seq, 1, dtype=np.float32)
    m = np.arange(1, heads + 1, dtype=np.float32) * np.float32(8.0 / heads)
    slopes = (np.float32(1.0) / np.float32(2.0) ** m).astype(np.float32)
    bias = slopes[:, None] * pos[None, :]
    rows = np.full((6, heads, seq), 0x3F80, dtype=np.uint16)
    for j in range(3):
        top = bias.view(np.uint32) >> 16
        rows[j] = top
        bias = bias - (top << 16).view(np.float32)
    return rows


def layer(nc, x, w_qkv, b_qkv, w_out, b_out, gate_w, w1, w3, w2, out):
    B, S, D = x.shape
    H, HD = 16, D // 16
    E, _, I = w1.shape
    TOPK = 8
    T = B * S // P
    TB = S // P
    KC = D // P
    G = 4
    UNITS = B * H // G
    NT = E + (B * S * TOPK - E) // P + 1
    EPS = 1e-5

    x_tiles = x.rearrange("b (t p) d -> p (b t) d", p=P)
    out_tiles = out.rearrange("b (t p) d -> (b t) p d", p=P)

    with ExitStack() as ctx:
        def sem(name):
            return ctx.enter_context(nc.semaphore(name))

        def dram(name, shape, dt):
            return nc.dram_tensor(name, shape, dt, kind="Internal").ap()

        k_rows = nc.inline_tensor(alibi_rows(H, S), "alibi_rows")
        k_rows = (k_rows if isinstance(k_rows, bass.AP) else k_rows.ap()).bitcast(BF16)
        stack_d = dram("stack_d", (B, 4, 8, 6 * HD, S), BF16)
        x1_d = dram("x1_d", (B * S, D), F32)
        y_d = dram("y_d", (NT * P, D), F32)

        def sb(name, shape, dt, c=ctx):
            return c.enter_context(nc.sbuf_tensor(name, shape, dt))

        w13 = sb("w13", [P, E, 2, KC, I], F32)
        X = sb("X", [P, T, D], F32)
        ident = sb("ident", [P, P], F32)
        identb = sb("identb", [P, P], BF16)
        stats = sb("stats", [P, T, 6], F32)
        mv = sb("mv", [P, T, 2], F32)
        rstd = sb("rstd", [P, T], F32)
        gateT = sb("gateT", [P, KC, E], F32)
        att = ExitStack()
        Qs = sb("Qs", [102, 4, G, S], BF16, att)
        Ks = sb("Ks", [102, 4, G, S], BF16, att)
        VH = HD + 1
        V = sb("V", [P, T, H * VH + 16], F32, att)
        WoT = sb("WoT", [P, 4, D], F32, att)
        maskA = sb("maskA", [P, P], BF16, att)
        maskB = sb("maskB", [P, P], BF16, att)
        sumsel = sb("sumsel", [P, P], F32, att)
        pro = ExitStack()
        w_raw = sb("w_raw", [P, 6, D], F32, pro)
        WT = sb("WT", [P, KC, 3 * D], F32, pro)
        xT = sb("xT", [P, KC, B * S], F32, pro)
        qk_f = sb("qk_f", [P, 2, S], F32, pro)
        qk_r = sb("qk_r", [P, 2, S], F32, pro)
        qk_p = sb("qk_p", [P, 2, 3, S], BF16, pro)
        bqk = sb("bqk", [P, 4], F32, pro)
        bv = sb("bv", [P, D], F32, pro)
        bo = sb("bo", [P, D], F32, pro)
        wo_raw = sb("wo_raw", [P, KC, D], F32, pro)
        wo_pad = sb("wo_pad", [P, KC, H * 32], F32, pro)
        gate_raw = sb("gate_raw", [E, D], F32, pro)
        pro.close()
        PT = sb("PT", [P, PRING, 2, S], F32, att)
        ctxT = sb("ctxT", [P, B, 4, S], F32, att)
        OT = sb("OT", [P, S], F32, att)
        Lr = sb("Lr", [P, S], F32, att)
        mx = sb("mx", [P, 2, TB, G], F32, att)
        mr = sb("mr", [P, 2, TB, G], F32, att)
        mx3 = sb("mx3", [P, 2, TB, 3, G], BF16, att)
        mT = sb("mT", [3 * G, 2, S], BF16, att)
        att.close()
        w2s = sb("w2s", [I, E, D], F32)
        x1T = sb("x1T", [P, 2, KC, P], F32)
        L = sb("L", [P, T, E], F32)
        Wc = sb("Wc", [P, T, E], F32)
        Sl = sb("Sl", [P, T, E], F32)
        Mk = sb("Mk", [P, T, E], BF16)
        top8 = sb("top8", [P, T, 8], F32)
        sl8 = sb("sl8", [P, T, 8], F32)
        slot_u = sb("slot_u", [P, T, 8], U32)
        slot_i = sb("slot_i", [P, T, 8], I32)
        part_i = sb("part_i", [P, 2, T, 8], I32)
        part_f = sb("part_f", [P, 2, T, 8], F32)
        upper = sb("upper", [P, P], BF16)
        onesb = sb("onesb", [P, P], BF16)
        onesf = sb("onesf", [P, E], F32)
        iota_f = sb("iota_f", [P, P], F32)
        iota_h = sb("iota_h", [P, P], F16)
        tok = sb("tok", [P, T], F32)
        cnt = sb("cnt", [P, 4, E], F32)
        cnt_i = sb("cnt_i", [P, 2, E], I32)
        te = sb("te", [P, E + 1], F32)
        te_row = sb("te_row", [1, NT], I32)
        ids = sb("ids", [P, NT], U32)
        zs = sb("zs", [P, 4, T], F32)
        wk = sb("wk", [P, T, 8], F32)
        junk = sb("junk", [P, E], F32)
        ohA = sb("ohA", [P, 4, P], F16)
        ohB = sb("ohB", [P, 4, P], F16)
        NG = 4
        gx = sb("gx", [P, NG, D], F32)
        gxT = sb("gxT", [P, 2, KC, P], F32)
        silu = sb("silu", [P, 2, I], F32)
        act_a = sb("act_a", [P, 2, I], F32)
        aT = sb("aT", [I, 2, P], F32)
        yo = sb("yo", [P, 2, D], F32)

        ps = ctx.enter_context(nc.psum_tensor("ps", [P, 8, 512], F32))

        x_in = [sem(f"x_in{b}") for b in range(B)]
        wqkv_in = sem("wqkv_in"); bias_in = sem("bias_in"); wo_in = sem("wo_in"); rows_in = sem("rows_in")
        consts = sem("consts"); pads = sem("pads")
        pe_job = sem("pe_job"); act_job = sem("act_job"); dve_job = sem("dve_job")
        part1 = sem("part1"); rest1 = sem("rest1"); part2 = sem("part2"); part3 = sem("part3")
        pieces_out = [sem(f"pieces_out{i}") for i in range(2)]
        stack_in = [sem(f"stack_in{i}") for i in range(4)]
        a_done = sem("a_done"); max_done = sem("max_done"); mx3_ready = sem("mx3_ready"); mT_ps = sem("mT_ps")
        mT_ready = sem("mT_ready"); mrow_in = [sem(f"mrow_in{i}") for i in range(4)]
        b_done = sem("b_done"); exp_done = sem("exp_done"); pv_done = sem("pv_done"); ot_ready = sem("ot_ready")
        sums_ps = sem("sums_ps"); ctx_ready = sem("ctx_ready"); proj_ps = sem("proj_ps"); y_ready = sem("y_ready")
        ln_sd = sem("ln_sd"); ln_var = sem("ln_var"); x1_ready = sem("x1_ready"); x1_out = sem("x1_out")
        w13_in = sem("w13_in"); w2_in = sem("w2_in")
        r_xT_ps = sem("r_xT_ps"); r_xT = sem("r_xT"); r_log_ps = sem("r_log_ps"); r_log = sem("r_log")
        mask_ready = sem("mask_ready"); pos_ps = sem("pos_ps"); shifted = sem("shifted"); exps = sem("exps")
        oh_ready = sem("oh_ready"); oh_used = sem("oh_used"); te_ready = sem("te_ready"); te_ps = sem("te_ps")
        te_out = sem("te_out"); ids_ready = sem("ids_ready")
        gx_in = [sem(f"gx_in{i}") for i in range(NG)]
        t_ps = sem("t_ps"); gxT_ready = sem("gxT_ready"); gu_ps = sem("gu_ps"); silu_ready = sem("silu_ready")
        a_ready = sem("a_ready"); aT_ps = sem("aT_ps"); aT_ready = sem("aT_ready"); y_ps = sem("y_ps")
        yo_ready = sem("yo_ready"); y_out = [sem(f"y_out{i}") for i in range(2)]
        row_in = [sem(f"row_in{i}") for i in range(8)]
        wk_ready = sem("wk_ready"); rows_used = sem("rows_used"); fin_ready = sem("fin_ready"); out_done = sem("out_done")
        dve_step = sem("dve_step"); pool_step = sem("pool_step")

        jobs = [("wT", 0), ("wT", 1), ("wT", 2)]
        for b in range(B):
            jobs += [("xT", b, c) for c in range(KC)] + [("qk", b, m) for m in (0, 2, 1, 3)]
        jobs += [("v", t) for t in range(T // 2)] + [("woT", 0), ("woT", 1), ("gT",)]
        on_act = {"wT", "woT", "gT"}
        qk_jobs = [j for j in jobs if j[0] == "qk"]

        def evacuated(eng, i):
            mine = jobs[i][0] in on_act
            n = sum((j[0] in on_act) == mine for j in jobs[:i + 1])
            eng.wait_ge(act_job if mine else dve_job, n)

        uses = []
        for u in range(2):
            uses += [("A", u * 8 + n) for n in range(8)]
        for u in range(UNITS):
            for i in range(TB):
                if u + 2 < UNITS:
                    uses += [("A", (u + 2) * 8 + 2 * i + hp) for hp in range(2)]
                uses += [("B", u * 8 + 2 * i + hp) for hp in range(2)]
        slot_of = {use: n % SLOTS for n, use in enumerate(uses)}

        def slot_free(eng, use):
            n = uses.index(use)
            if n >= SLOTS:
                kind, i = uses[n - SLOTS]
                eng.wait_ge(max_done if kind == "A" else exp_done, i + 1)

        def slot(use):
            return ps[:, 2 * slot_of[use]:2 * slot_of[use] + 2, :]

        def misc_free(eng, kind, i):
            n = misc.index((kind, i))
            if n:
                k, j = misc[n - 1]
                eng.wait_ge({"T": mT_ready, "L": ctx_ready, "O": y_ready}[k], j + 1)

        misc = [("T", 0)]
        for u in range(UNITS):
            for i in range(TB):
                if i == 0 and u + 1 < UNITS:
                    misc.append(("T", u + 1))
                if i == 2 and u >= 1:
                    misc.append(("L", u - 1))
                if u == 5:
                    misc.append(("O", i))
        misc.append(("L", UNITS - 1))
        misc += [("O", TB + i) for i in range(TB)]

        block = ctx.enter_context(nc.Block())

        rows = w13[:, 0:8, :, :, :].rearrange("p e j c i -> p e (j c i)")[:, :, 0:D]

        @block.sync
        def _(sp):
            sp.dma_start(w_raw[:, :, :], w_qkv.rearrange("(r p) d -> p r d", p=P)).then_inc(wqkv_in, 16)
            for b in range(B):
                sp.dma_start(X[:, b * TB:(b + 1) * TB, :], x_tiles[:, b * TB:(b + 1) * TB, :]).then_inc(x_in[b], 16)
            sp.dma_start(bqk[:, :], b_qkv[0:2 * D].rearrange("(c p) -> p c", p=P),
                         allow_slow_non_contiguous=True).then_inc(bias_in, 16)
            sp.dma_start(bv[:, :], b_qkv[2 * D:3 * D].partition_broadcast(P)).then_inc(bias_in, 16)
            sp.dma_start(bo[:, :], b_out.partition_broadcast(P)).then_inc(bias_in, 16)
            sp.dma_start(wo_raw[:, :, :], w_out.rearrange("(c p) d -> p c d", p=P)).then_inc(wo_in, 16)
            sp.dma_start(gate_raw[:, :], gate_w).then_inc(wo_in, 16)
            sp.dma_start(Ks[96:102, :, :, :], k_rows.rearrange("r (s g) t -> r s g t", s=4)).then_inc(rows_in, 16)
            sp.dma_start(Qs[96:99, :, :, :], k_rows[3:6].rearrange("r (s g) t -> r s g t", s=4)).then_inc(rows_in, 16)

            def write_pieces(r):
                _, b, m = qk_jobs[r]
                order = (0, 0, 0, 1, 1, 2) if m < 2 else (0, 1, 2, 0, 1, 0)
                waits = {0: part1, 1: part2, 2: part3}
                for piece in range(3):
                    sp.wait_ge(waits[piece], r + 1)
                    for j in range(6):
                        if order[j] == piece:
                            sp.dma_start(stack_d[b, m, :, j * HD:(j + 1) * HD, :],
                                         qk_p[:, r % 2, piece, :]).then_inc(pieces_out[r % 2], 16)

            def read_stack(u):
                b, g = divmod(u, 4)
                for r in (4 * b + 2 * (g // 2), 4 * b + 2 * (g // 2) + 1):
                    sp.wait_ge(pieces_out[r % 2], 96 * (r // 2 + 1))
                if u >= 4:
                    sp.wait_ge(b_done, (u - 3) * 8)
                h0 = G * (g % 2)
                for dst, m in ((Qs, g // 2), (Ks, 2 + g // 2)):
                    sp.dma_start(dst[0:96, g, :, :],
                                 stack_d[b, m, h0:h0 + G, :, :].rearrange("h r t -> r h t")).then_inc(stack_in[g], 16)

            def load_w13(n):
                e = slice(4 * n, 4 * n + 4)
                for j, w in enumerate((w1, w3)):
                    sp.dma_start(w13[:, e, j, :, :].rearrange("p e c i -> p e (c i)"),
                                 w[e].rearrange("e (p c) i -> p e (c i)", c=KC)).then_inc(w13_in, 16)

            for r in range(len(qk_jobs)):
                write_pieces(r)
                if r % 2 == 0 and 2 <= r <= 4:
                    read_stack(r - 2)
                    read_stack(r - 1)
            for u in range(4, UNITS):
                for n in range(4):
                    load_w13(4 * (u - 4) + n)
                read_stack(u)
            sp.wait_ge(y_ready, T)
            sp.wait_ge(x1_ready, T)
            for n in range(8):
                sp.dma_start(w2s[:, 8 * n:8 * n + 8, :], w2[8 * n:8 * n + 8].rearrange("e i d -> i e d")).then_inc(w2_in, 16)
            sp.dma_start(x1_d.rearrange("(t p) d -> p t d", p=P), X[:, :, :]).then_inc(x1_out, 16)
            with sp.Fori(0, NT // 2) as n:
                for i in range(2):
                    sp.wait_ge(yo_ready, 2 * n + (i + 1))
                    sp.dma_start(y_d[bass.ds((2 * n + i) * P, P), :], yo[:, i, :]).then_inc(y_out[i], 16)
            for t in range(T):
                sp.wait_ge(fin_ready, t + 1)
                sp.dma_start(out_tiles[t], X[:, t, :]).then_inc(out_done, 16)
            sp.wait_ge(out_done, 16 * T)

        @block.gpsimd
        def _(pool):
            n = 0

            def step(ins):
                nonlocal n
                n += 1
                ins.then_inc(pool_step, 1)
                pool.wait_ge(pool_step, n)

            step(pool.memset(ident[:, :], 1.0))
            step(pool.affine_select(out=ident[:, :], in_=ident[:, :], compare_op=ALU.is_equal, fill=0.0, base=0,
                                    pattern=[[-1, P]], channel_multiplier=1))
            step(pool.memset(wo_pad[:, :, :], 0.0))
            pool.tensor_copy(identb[:, :], ident[:, :]).then_inc(consts, 1)
            step(pool.memset(maskA[:, :], 0.0))
            step(pool.memset(maskB[:, :], 0.0))
            pool.affine_select(out=maskA[:, :], in_=maskA[:, :], compare_op=ALU.is_ge, fill=NEG, base=0,
                               pattern=[[-1, P]], channel_multiplier=1).then_inc(consts, 1)
            pool.affine_select(out=maskB[:, :], in_=maskB[:, :], compare_op=ALU.is_ge, fill=NEG, base=0,
                               pattern=[[1, P]], channel_multiplier=-1).then_inc(consts, 1)
            step(pool.memset(sumsel[:, :], 1.0))
            pool.affine_select(out=sumsel[:, :].rearrange("p (a b) -> p a b", a=4),
                               in_=sumsel[:, :].rearrange("p (a b) -> p a b", a=4), compare_op=ALU.is_equal, fill=0.0,
                               base=-16, pattern=[[-32, 4], [0, 32]], channel_multiplier=1).then_inc(consts, 1)
            pool.memset(V[:, :, :], 1.0).then_inc(consts, 1)
            pool.wait_ge(wo_in, 32)
            pool.tensor_copy(wo_pad[:, :, :].rearrange("p c (h d) -> p c h d", d=32)[:, :, :, 0:HD],
                             wo_raw[:, :, :].rearrange("p c (h d) -> p c h d", d=HD)).then_inc(pads, 1)
            for r in range(len(qk_jobs)):
                pool.wait_ge(part2, r + 1)
                if r >= 2:
                    pool.wait_ge(pieces_out[r % 2], 96 * (r // 2))
                pool.tensor_tensor(qk_p[:, r % 2, 2, :], qk_r[:, r % 2, :], qk_p[:, r % 2, 1, :],
                                   ALU.subtract).then_inc(part3, 1)
            for u in range(UNITS):
                pool.wait_ge(mT_ready, u + 1)
                for j in range(3):
                    pool.dma_start(Qs[99 + j:100 + j, u % 4, :, :], mT[G * j:G * j + G, u % 2, :]).then_inc(mrow_in[u % 4], 16)
            pool.wait_ge(x1_ready, T)
            step(pool.memset(upper[:, :], 1.0))
            pool.affine_select(out=upper[:, :], in_=upper[:, :], compare_op=ALU.is_gt, fill=0.0, base=0,
                               pattern=[[1, P]], channel_multiplier=-1).then_inc(consts, 1)
            pool.memset(onesb[:, :], 1.0).then_inc(consts, 1)
            pool.memset(onesf[:, :], 1.0).then_inc(consts, 1)
            pool.iota(slot_i[:, :, :].rearrange("p a b -> p (a b)")[:, 0:T], pattern=[[P, T]], base=0,
                      channel_multiplier=1).then_inc(pool_step, 1)
            pool.iota(ids[:, :].bitcast(I32), pattern=[[1, NT]], base=0, channel_multiplier=0).then_inc(pool_step, 1)
            n += 2
            pool.wait_ge(pool_step, n)
            pool.tensor_copy(tok[:, :], slot_i[:, :, :].rearrange("p a b -> p (a b)")[:, 0:T]).then_inc(consts, 1)
            pool.tensor_copy(iota_h[:, :], ids[:, :].bitcast(I32)).then_inc(consts, 1)
            pool.wait_ge(x1_out, 16)

            pool.wait_ge(ids_ready, 1)
            for i in range(NT):
                if i >= NG:
                    pool.wait_ge(t_ps, i + 1 - NG)
                pool.indirect_dma_start(gx[:, i % NG, :], None, x1_d,
                                        bass.IndirectOffsetOnAxis(ids[:, i:i + 1], 0)).then_inc(gx_in[i % NG], 16)
            for i in range(2):
                pool.wait_ge(y_out[i], 16 * (NT // 2))
            pool.wait_ge(t_ps, NT)
            for n in range(T * TOPK):
                t, k = divmod(n, TOPK)
                if n >= 8:
                    pool.wait_ge(rows_used, n - 7)
                pool.indirect_dma_start(rows[:, n % 8, :], None, y_d,
                                        bass.IndirectOffsetOnAxis(slot_u[:, t, k:k + 1], 0)).then_inc(row_in[n % 8], 16)

        @block.scalar
        def _(act):
            def job(i):
                kind = jobs[i][0]
                bank = ps[:, i % 8, :]
                act.wait_ge(pe_job, i + 1)
                if kind == "wT":
                    g = jobs[i][1]
                    act.copy(WT[:, :, :].rearrange("p c n -> p (c n)")[:, 512 * g:512 * g + 512], bank).then_inc(act_job, 1)
                elif kind == "woT":
                    g = jobs[i][1]
                    act.copy(WoT[:, :, :].rearrange("p g n -> p (g n)")[:, 512 * g:512 * g + 512], bank).then_inc(act_job, 1)
                else:
                    act.copy(gateT[:, :, :].rearrange("p c e -> p (c e)"), bank[:, 0:KC * E]).then_inc(act_job, 1)

            r = 0
            for i, j in enumerate(jobs):
                if j[0] in on_act:
                    job(i)
                elif j[0] == "qk":
                    if r >= 2:
                        act.wait_ge(pieces_out[r % 2], 96 * (r // 2))
                    act.wait_ge(dve_job, sum(q[0] not in on_act for q in jobs[:i + 1]))
                    act.copy(qk_p[:, r % 2, 0, :], qk_f[:, r % 2, :]).then_inc(part1, 1)
                    act.wait_ge(rest1, r + 1)
                    act.copy(qk_p[:, r % 2, 1, :], qk_r[:, r % 2, :]).then_inc(part2, 1)
                    r += 1

            def max_rows(u):
                act.wait_ge(mT_ps, u + 1)
                if u >= 2:
                    act.wait_ge(mrow_in[(u - 2) % 4], 48 * ((u - 2) // 4 + 1))
                act.copy(mT[:, u % 2, :], ps[0:3 * G, 7, :]).then_inc(mT_ready, 1)

            def probs(u, kb, hp):
                n = u * 8 + 2 * kb + hp
                act.wait_ge(b_done, n + 1)
                if n >= PRING:
                    act.wait_ge(pv_done, n - PRING + 1)
                N = S - kb * P
                act.activation(PT[:, n % PRING, :, 0:N], slot(("B", n))[:, :, 0:N], ACT.Exp).then_inc(exp_done, 1)

            def heads_out(u):
                act.wait_ge(pv_done, 8 * (u + 1))
                if u >= 1:
                    act.wait_ge(ctx_ready, u)
                act.copy(OT[:, :], ps[:, 6, :]).then_inc(ot_ready, 1)

            act.wait_ge(pe_job, len(jobs))
            act.wait_ge(part3, len(qk_jobs))
            for q in pieces_out:
                act.wait_ge(q, 96 * len(qk_jobs) // 2)
            max_rows(0)
            for u in range(UNITS):
                if u + 1 < UNITS:
                    max_rows(u + 1)
                for kb in range(TB):
                    for hp in range(2):
                        probs(u, kb, hp)
                    if kb == 0 and u >= 1:
                        heads_out(u - 1)
            heads_out(UNITS - 1)
            act.wait_ge(ln_var, 1)
            act.activation(rstd[:, :], rstd[:, :], ACT.Sqrt).then_inc(ln_sd, 1)
            for t in range(T):
                act.wait_ge(r_xT_ps, t + 1)
                if t >= 2:
                    act.wait_ge(r_log_ps, t - 1)
                act.copy(x1T[:, t % 2, :, :].rearrange("p c n -> p (c n)"), ps[:, t % 2, 0:KC * P]).then_inc(r_xT, 1)
            act.wait_ge(shifted, 1)
            act.activation(Wc[:, :, :], Wc[:, :, :], ACT.Exp).then_inc(exps, 1)
            act.wait_ge(te_ps, 1)
            act.copy(te_row[:, :], ps[0:1, 6, 0:NT]).then_inc(te_out, 1)
            act.wait_ge(oh_used, T * TOPK)
            act.copy(ids[:, :], ps[:, 7, 0:NT]).then_inc(ids_ready, 1)

            def gate(i, b, j):
                act.wait_ge(gu_ps, i + 1)
                if j is not None:
                    act.wait_ge(a_ready, i - 1)
                act.activation(silu[:, b, :], ps[:, 2 + b, 0:I], ACT.Silu).then_inc(silu_ready, 1)

            def y_store(i, b, j):
                act.wait_ge(y_ps, i + 1)
                if j is not None:
                    act.wait_ge(y_out[b], 16 * j)
                act.copy(yo[:, b, :], ps[:, 6 + b, 0:D]).then_inc(yo_ready, 1)

            gate(0, 0, None); gate(1, 1, None)
            gate(2, 0, 0); y_store(0, 0, None)
            gate(3, 1, 0); y_store(1, 1, None)
            with act.Fori(2, NT // 2) as j:
                for i in range(2):
                    gate(2 * j + i, i, 0)
                    y_store(2 * j + (i - 2), i, j - 1)
            for i in range(NT - 2, NT):
                y_store(i, i % 2, i // 2)
            act.wait_ge(ln_var, 2)
            for t in range(T):
                act.wait_ge(ln_var, t + 2)
                act.activation(rstd[:, t:t + 1], rstd[:, t:t + 1], ACT.Sqrt).then_inc(ln_sd, 1)

        @block.vector
        def _(dve):
            n_step = 0

            def step(ins):
                nonlocal n_step
                n_step += 1
                ins.then_inc(dve_step, 1)
                dve.wait_ge(dve_step, n_step)

            def rest(r):
                dve.wait_ge(part1, r + 1)
                if r >= 2:
                    dve.wait_ge(part3, r - 1)
                dve.tensor_tensor(qk_r[:, r % 2, :], qk_f[:, r % 2, :], qk_p[:, r % 2, 0, :],
                                  ALU.subtract).then_inc(rest1, 1)

            dve.wait_ge(bias_in, 48)
            r = 0
            for i, j in enumerate(jobs):
                if j[0] in on_act:
                    continue
                bank = ps[:, i % 8, :]
                dve.wait_ge(pe_job, i + 1)
                if j[0] == "xT":
                    dve.tensor_copy(xT[:, j[2], j[1] * S:(j[1] + 1) * S], bank).then_inc(dve_job, 1)
                elif j[0] == "qk":
                    b, m = j[1:]
                    if r >= 2:
                        dve.wait_ge(rest1, r - 1)
                    dve.tensor_scalar(qk_f[:, r % 2, :], bank, bqk[:, m:m + 1], 0.25 if m < 2 else 1.0,
                                      ALU.add, ALU.mult).then_inc(dve_job, 1)
                    if r >= 1:
                        rest(r - 1)
                    r += 1
                    if r == len(qk_jobs):
                        rest(r - 1)
                elif j[0] == "v":
                    for t in (2 * j[1], 2 * j[1] + 1):
                        if t == 0:
                            dve.wait_ge(consts, 5)
                        ins = dve.tensor_tensor(V[:, t, 0:H * VH].rearrange("p (h d) -> p h d", d=VH)[:, :, 0:HD],
                                                bank[:, (t % 2) * D:(t % 2) * D + D].rearrange("p (h d) -> p h d", d=HD),
                                                bv[:, :].rearrange("p (h d) -> p h d", d=HD), ALU.add)
                    ins.then_inc(dve_job, 1)
            for t in range(T):
                ins = dve.tensor_tensor(X[:, t, :], X[:, t, :], bo[:, :], ALU.add)
            step(ins)

            def row_max(u, i):
                for hp in range(2):
                    n = u * 8 + 2 * i + hp
                    dve.wait_ge(a_done, n + 1)
                    if i == 0 and hp == 0 and u >= 2:
                        dve.wait_ge(mT_ps, u - 1)
                    dve.tensor_reduce(mx[:, u % 2, i, 2 * hp:2 * hp + 2], slot(("A", n))[:, :, 0:(i + 1) * P],
                                      AX.X, ALU.max).then_inc(max_done, 1)

            def max_parts(u):
                m, rr, m3 = mx[:, u % 2], mr[:, u % 2], mx3[:, u % 2]
                dve.wait_ge(max_done, 8 * (u + 1))
                step(dve.tensor_scalar(m3[:, :, 0, :], m, -1.0, None, ALU.mult))
                step(dve.scalar_tensor_tensor(out=rr, in0=m, scalar=-1.0, in1=m3[:, :, 0, :], op0=ALU.mult, op1=ALU.subtract))
                step(dve.tensor_copy(m3[:, :, 1, :], rr))
                dve.tensor_tensor(m3[:, :, 2, :], rr, m3[:, :, 1, :], ALU.subtract).then_inc(mx3_ready, 1)

            def normalise(u):
                b, g = divmod(u, 4)
                dve.wait_ge(sums_ps, u + 1)
                step(dve.reciprocal(Lr[:, :], ps[:, 7, :]))
                dve.tensor_tensor(ctxT[:, b, g, :], OT[:, :], Lr[:, :], ALU.mult).then_inc(ctx_ready, 1)

            def residual(t):
                dve.wait_ge(proj_ps, t + 1)
                dve.tensor_tensor(X[:, t, :], ps[:, 7, 0:D], X[:, t, :], ALU.add).then_inc(y_ready, 1)

            dve.wait_ge(pe_job, len(jobs))
            dve.wait_ge(act_job, sum(j[0] in on_act for j in jobs))
            dve.wait_ge(part3, len(qk_jobs))
            for q in pieces_out:
                dve.wait_ge(q, 96 * len(qk_jobs) // 2)
            for u in range(2):
                for i in range(TB):
                    row_max(u, i)
                max_parts(u)
            for u in range(UNITS):
                for i in range(TB):
                    if u + 2 < UNITS:
                        row_max(u + 2, i)
                    if i == 2 and u >= 1:
                        normalise(u - 1)
                    if u == 5:
                        residual(i)
                if u + 2 < UNITS:
                    max_parts(u + 2)
            normalise(UNITS - 1)
            for i in range(TB):
                residual(TB + i)

            def statistics(t):
                step(dve.bn_stats(stats[:, t, :], X[:, t, :]))
                dve.bn_aggr(mv[:, t, :], stats[:, t, :])

            dve.wait_ge(y_ready, T)
            for t in range(T):
                step(dve.bn_stats(stats[:, t, :], X[:, t, :]))
            for t in range(T):
                ins = dve.bn_aggr(mv[:, t, :], stats[:, t, :])
            step(ins)
            dve.tensor_scalar(rstd[:, :], mv[:, :, 1], EPS, None, ALU.add).then_inc(ln_var, 1)
            dve.wait_ge(ln_sd, 1)
            step(dve.reciprocal(rstd[:, :], rstd[:, :]))
            for t in range(T):
                dve.tensor_scalar(X[:, t, :], X[:, t, :], mv[:, t, 0:1], rstd[:, t:t + 1],
                                  ALU.subtract, ALU.mult).then_inc(x1_ready, 1)
            for t in range(T):
                dve.wait_ge(r_log_ps, t + 1)
                step(dve.tensor_copy(L[:, t, :], ps[:, 2 + t % 2, 0:E]))
                step(dve.max(top8[:, t, :], L[:, t, :]))
                dve.match_replace(out=Sl[:, t, :], in_to_replace=top8[:, t, :], in_values=L[:, t, :],
                                  imm_value=-3.0e38).then_inc(r_log, 1)
            dve.wait_ge(r_log, T)
            dve.tensor_tensor(Mk[:, :, :], Sl[:, :, :], L[:, :, :], ALU.not_equal).then_inc(mask_ready, 1)
            dve.tensor_tensor(Wc[:, :, :], L[:, :, :], top8[:, :, 0:1].broadcast_to((P, T, E)), ALU.subtract).then_inc(shifted, 1)
            dve.wait_ge(pos_ps, 2)
            step(dve.tensor_scalar(cnt_i[:, 0, :], ps[:, 5, 0:E], float(P - 1), None, ALU.add))
            step(dve.tensor_scalar(cnt_i[:, 1, :], cnt_i[:, 0, :], 7, None, ALU.logical_shift_right))
            step(dve.tensor_copy(cnt[:, 0, :], cnt_i[:, 1, :]))
            dve.wait_ge(consts, 10)
            step(dve.tensor_tensor_scan(cnt[:, 1, :], onesf[:, :], cnt[:, 0, :], 0.0, ALU.mult, ALU.add))
            step(dve.tensor_tensor(cnt[:, 2, :], cnt[:, 1, :], cnt[:, 0, :], ALU.subtract))
            step(dve.tensor_scalar(cnt[:, 3, :], cnt[:, 2, :], float(P), 1.0, ALU.mult, ALU.add))
            step(dve.tensor_scalar(te[:, 0:E], cnt[:, 1, :], tok[:, 0:1], None, ALU.is_le))
            step(dve.tensor_reduce(te[:, E:E + 1], te[:, 0:E], AX.X, ALU.add))
            dve.tensor_scalar(te[:, 0:1], te[:, E:E + 1], float(E - 1), None, ALU.min).then_inc(te_ready, 1)
            step(dve.tensor_tensor(Sl[:, :, :], ps[:, 4, :].rearrange("p (t e) -> p t e", e=E),
                                   cnt[:, 3:4, :].broadcast_to((P, T, E)), ALU.add))
            step(dve.tensor_tensor(Sl[:, :, :], Sl[:, :, :], Mk[:, :, :], ALU.mult))
            for t in range(T):
                ins = dve.max(sl8[:, t, :], Sl[:, t, :])
            step(ins)
            step(dve.tensor_scalar(slot_i[:, :, :], sl8[:, :, :], -1.0, None, ALU.add))
            dve.tensor_copy(slot_u[:, :, :], slot_i[:, :, :])
            dve.tensor_scalar(part_i[:, 0], slot_i[:, :, :], P - 1, None, ALU.bitwise_and)
            step(dve.tensor_scalar(part_i[:, 1], slot_i[:, :, :], 7, None, ALU.logical_shift_right))
            step(dve.tensor_copy(part_f[:, :, :, :], part_i[:, :, :, :]))
            for n in range(T * TOPK):
                t, k = divmod(n, TOPK)
                if n >= 4:
                    dve.wait_ge(oh_used, n - 3)
                dve.tensor_scalar(ohA[:, n % 4, :], iota_h[:, :], part_f[:, 0, t, k:k + 1], None, ALU.is_equal)
                dve.tensor_scalar(ohB[:, n % 4, :], iota_h[:, :], part_f[:, 1, t, k:k + 1], tok[:, t:t + 1],
                                  ALU.is_equal, ALU.mult).then_inc(oh_ready, 1)
            dve.wait_ge(exps, 1)
            step(dve.tensor_reduce(zs[:, 0, :], Wc[:, :, :], AX.X, ALU.add))
            step(dve.tensor_tensor(Wc[:, :, :], Wc[:, :, :], Mk[:, :, :], ALU.mult))
            step(dve.tensor_reduce(zs[:, 1, :], Wc[:, :, :], AX.X, ALU.add))
            step(dve.scalar_tensor_tensor(out=zs[:, 2, :], in0=zs[:, 0, :], scalar=1e-20, in1=zs[:, 1, :],
                                          op0=ALU.mult, op1=ALU.add))
            step(dve.reciprocal(zs[:, 3, :], zs[:, 2, :]))
            for t in range(T):
                ins = dve.tensor_scalar(Wc[:, t, :], Wc[:, t, :], zs[:, 3, t:t + 1], None, ALU.mult)
            step(ins)

            def rows_T(i, b, again):
                dve.wait_ge(t_ps, i + 1)
                if again:
                    dve.wait_ge(gu_ps, i - 1)
                dve.tensor_copy(gxT[:, b, :, :].rearrange("p c n -> p (c n)"), ps[:, b, 0:KC * P]).then_inc(gxT_ready, 1)

            def product(i, b, again):
                dve.wait_ge(silu_ready, i + 1)
                if again:
                    dve.wait_ge(aT_ps, i - 1)
                dve.tensor_tensor(act_a[:, b, :], silu[:, b, :], ps[:, 2 + b, I:2 * I], ALU.mult).then_inc(a_ready, 1)

            def hidden_T(i, b, again):
                dve.wait_ge(aT_ps, i + 1)
                if again:
                    dve.wait_ge(y_ps, i - 1)
                dve.tensor_copy(aT[:, b, :], ps[0:I, 4 + b, 0:P]).then_inc(aT_ready, 1)

            rows_T(0, 0, False)
            rows_T(1, 1, False); product(0, 0, False)
            rows_T(2, 0, True); hidden_T(0, 0, False); product(1, 1, False)
            rows_T(3, 1, True); hidden_T(1, 1, False); product(2, 0, True)
            with dve.Fori(2, NT // 2) as j:
                for i in range(2):
                    rows_T(2 * j + i, i, True)
                    hidden_T(2 * j + (i - 2), i, True)
                    product(2 * j + (i - 1), 1 - i, True)
            hidden_T(NT - 2, 0, True)
            product(NT - 1, 1, True)
            hidden_T(NT - 1, 1, True)

            for t in range(T):
                for k in range(TOPK):
                    if k or t:
                        dve.wait_ge(wk_ready, t * TOPK + k)
                    dve.scalar_tensor_tensor(out=junk[:, :], in0=Sl[:, t, :], scalar=sl8[:, t, k:k + 1], in1=Wc[:, t, :],
                                             op0=ALU.is_equal, op1=ALU.mult, accum_out=wk[:, t, k:k + 1]).then_inc(wk_ready, 1)
            dve.wait_ge(wk_ready, T * TOPK)
            for t in range(T):
                for k in range(TOPK):
                    n = t * TOPK + k
                    dve.wait_ge(row_in[n % 8], 16 * (n // 8 + 1))
                    if n:
                        dve.wait_ge(rows_used, n)
                    dve.scalar_tensor_tensor(out=X[:, t, :], in0=rows[:, n % 8, :], scalar=wk[:, t, k:k + 1], in1=X[:, t, :],
                                             op0=ALU.mult, op1=ALU.add).then_inc(rows_used, 1)
                dve.wait_ge(rows_used, (t + 1) * TOPK)
                step(dve.bn_stats(stats[:, t, :], X[:, t, :]))
                step(dve.bn_aggr(mv[:, t, :], stats[:, t, :]))
                dve.tensor_scalar(rstd[:, t:t + 1], mv[:, t, 1:2], EPS, None, ALU.add).then_inc(ln_var, 1)
                dve.wait_ge(ln_sd, t + 2)
                step(dve.reciprocal(rstd[:, t:t + 1], rstd[:, t:t + 1]))
                dve.tensor_scalar(X[:, t, :], X[:, t, :], mv[:, t, 0:1], rstd[:, t:t + 1],
                                  ALU.subtract, ALU.mult).then_inc(fin_ready, 1)

        @block.tensor
        def _(pe):
            pe.wait_ge(consts, 1)
            pe.wait_ge(wqkv_in, 16)
            for i, j in enumerate(jobs):
                kind, bank = j[0], ps[:, i % 8, :]
                if i >= 8:
                    evacuated(pe, i - 8)
                if kind == "wT":
                    for n in range(4):
                        c, r = divmod(4 * j[1] + n, 6)
                        last = pe.transpose(bank[:, n * P:(n + 1) * P], w_raw[:, r, c * P:(c + 1) * P], ident[:, :])
                elif kind == "xT":
                    b, c = j[1:]
                    pe.wait_ge(x_in[b], 16)
                    for t in range(TB):
                        last = pe.transpose(bank[:, t * P:(t + 1) * P], X[:, b * TB + t, c * P:(c + 1) * P], ident[:, :])
                elif kind == "qk":
                    b, m = j[1:]
                    if m == 0:
                        evacuated(pe, 2)
                        evacuated(pe, jobs.index(("xT", b, KC - 1)))
                    for c in range(KC):
                        last = pe.matmul(bank, WT[:, c, m * P:(m + 1) * P], xT[:, c, b * S:(b + 1) * S],
                                         start=(c == 0), stop=(c == KC - 1))
                elif kind == "v":
                    for t in (2 * j[1], 2 * j[1] + 1):
                        for c in range(KC):
                            last = pe.matmul(bank[:, (t % 2) * D:(t % 2) * D + D], xT[:, c, t * P:(t + 1) * P],
                                             WT[:, c, 2 * D:3 * D], start=(c == 0), stop=(c == KC - 1))
                elif kind == "woT":
                    pe.wait_ge(pads, 1)
                    for n in range(4):
                        g, c = divmod(4 * j[1] + n, KC)
                        last = pe.transpose(bank[:, n * P:(n + 1) * P], wo_pad[:, c, g * P:(g + 1) * P], ident[:, :])
                else:
                    for c in range(KC):
                        last = pe.transpose(bank[:, c * E:(c + 1) * E], gate_raw[:, c * P:(c + 1) * P], ident[0:E, 0:E])
                last.then_inc(pe_job, 1)
            for i in range(len(jobs) - 8, len(jobs)):
                evacuated(pe, i)
            pe.wait_ge(consts, 5)
            pe.wait_ge(rows_in, 32)

            def scores_A(u, i):
                s = u % 4
                if i == 0:
                    pe.wait_ge(stack_in[s], 32 * (u // 4 + 1))
                for hp in range(2):
                    n = u * 8 + 2 * i + hp
                    slot_free(pe, ("A", n))
                    dst = slot(("A", n))
                    for j in range(2):
                        h = 2 * hp + j
                        pe.matmul(dst[:, j, 0:(i + 1) * P], Qs[0:99, s, h, i * P:(i + 1) * P], Ks[0:99, s, h, 0:(i + 1) * P],
                                  start=True, stop=False)
                        last = pe.matmul(dst[:, j, i * P:(i + 1) * P], identb[:, :], maskA[:, :], start=False, stop=True)
                    last.then_inc(a_done, 1)

            def scores_B(u, kb):
                s = u % 4
                if kb == 0:
                    pe.wait_ge(mrow_in[s], 48 * (u // 4 + 1))
                for hp in range(2):
                    n = u * 8 + 2 * kb + hp
                    slot_free(pe, ("B", n))
                    dst = slot(("B", n))
                    for j in range(2):
                        h = 2 * hp + j
                        pe.matmul(dst[:, j, 0:S - kb * P], Ks[:, s, h, kb * P:(kb + 1) * P], Qs[:, s, h, kb * P:S],
                                  start=True, stop=False)
                        last = pe.matmul(dst[:, j, 0:P], identb[:, :], maskB[:, :], start=False, stop=True)
                    last.then_inc(b_done, 1)

            def values(u, kb):
                b, g = divmod(u, 4)
                if kb == 0 and u:
                    pe.wait_ge(ot_ready, u)
                for hp in range(2):
                    n = u * 8 + 2 * kb + hp
                    pe.wait_ge(exp_done, n + 1)
                    for j in range(2):
                        h = 2 * hp + j
                        last = pe.matmul(ps[32 * h:32 * h + 32, 6, kb * P:S],
                                         V[:, b * TB + kb, (G * g + h) * VH:(G * g + h) * VH + 32],
                                         PT[:, n % PRING, j, 0:S - kb * P], start=(kb == 0), stop=(kb == TB - 1))
                    last.then_inc(pv_done, 1)

            def max_rows(u):
                pe.wait_ge(mx3_ready, u + 1)
                misc_free(pe, "T", u)
                for i in range(TB):
                    last = pe.matmul(ps[0:3 * G, 7, i * P:(i + 1) * P],
                                     mx3[:, u % 2, i, :, :].rearrange("p j h -> p (j h)"), identb[:, :], start=True, stop=True)
                last.then_inc(mT_ps, 1)

            def sums(u):
                pe.wait_ge(ot_ready, u + 1)
                misc_free(pe, "L", u)
                pe.matmul(ps[:, 7, :], sumsel[:, :], OT[:, :], start=True, stop=True).then_inc(sums_ps, 1)

            def project(t):
                b = t // TB
                pe.wait_ge(ctx_ready, 4 * (b + 1))
                misc_free(pe, "O", t)
                for g in range(4):
                    last = pe.matmul(ps[:, 7, 0:D], ctxT[:, b, g, (t % TB) * P:(t % TB + 1) * P], WoT[:, g, :],
                                     start=(g == 0), stop=(g == 3))
                last.then_inc(proj_ps, 1)

            for i in range(TB):
                scores_A(0, i)
            for i in range(TB):
                scores_A(1, i)
            max_rows(0)
            for u in range(UNITS):
                for i in range(TB):
                    if i == 0 and u + 1 < UNITS:
                        max_rows(u + 1)
                    if u + 2 < UNITS:
                        scores_A(u + 2, i)
                    scores_B(u, i)
                    if i:
                        values(u, i - 1)
                    if i == 2 and u >= 1:
                        sums(u - 1)
                    if u == 5:
                        project(i)
                values(u, TB - 1)
            sums(UNITS - 1)
            for i in range(TB):
                project(TB + i)

            pe.wait_ge(y_ready, T)
            for t in range(T):
                pe.wait_ge(x1_ready, t + 1)
                if t >= 2:
                    pe.wait_ge(r_xT, t - 1)
                for c in range(KC):
                    last = pe.transpose(ps[:, t % 2, c * P:(c + 1) * P], X[:, t, c * P:(c + 1) * P], ident[:, :])
                last.then_inc(r_xT_ps, 1)
                pe.wait_ge(r_xT, t + 1)
                if t >= 2:
                    pe.wait_ge(r_log, t - 1)
                for c in range(KC):
                    last = pe.matmul(ps[:, 2 + t % 2, 0:E], x1T[:, t % 2, c, :], gateT[:, c, :], start=(c == 0), stop=(c == KC - 1))
                last.then_inc(r_log_ps, 1)
            pe.wait_ge(consts, 10)
            pe.wait_ge(mask_ready, 1)
            for t in range(T):
                for q in range(t + 1):
                    last = pe.matmul(ps[:, 4, t * E:(t + 1) * E], upper[:, :] if q == t else onesb[:, :], Mk[:, q, :],
                                     start=(q == 0), stop=(q == t))
            last.then_inc(pos_ps, 1)
            for q in range(T):
                last = pe.matmul(ps[:, 5, 0:E], onesb[:, :], Mk[:, q, :], start=(q == 0), stop=(q == T - 1))
            last.then_inc(pos_ps, 1)
            pe.wait_ge(te_ready, 1)
            pe.matmul(ps[0:1, 6, 0:NT], te[:, 0:1], ident[:, :], start=True, stop=True).then_inc(te_ps, 1)
            for n in range(T * TOPK):
                pe.wait_ge(oh_ready, n + 1)
                pe.matmul(ps[:, 7, 0:NT], ohA[:, n % 4, :], ohB[:, n % 4, :], start=(n == 0),
                          stop=(n == T * TOPK - 1)).then_inc(oh_used, 1)
            pe.wait_ge(te_out, 1)
            pe.wait_ge(w13_in, 16 * 2 * E // 4)

            def rows_T(i, g, b, n, again):
                pe.wait_ge(gx_in[g], n)
                if again:
                    pe.wait_ge(gxT_ready, i - 1)
                v = gx[:, g, :].rearrange("p (n c) -> p c n", c=KC)
                for c in range(KC):
                    last = pe.transpose(ps[:, b, c * P:(c + 1) * P], v[:, c, :], ident[:, :])
                last.then_inc(t_ps, 1)

            def gate_up(i, b, again):
                e = pe.value_load(te_row[0:1, bass.ds(i, 1)], min_val=0, max_val=E - 1)
                pe.wait_ge(gxT_ready, i + 1)
                if again:
                    pe.wait_ge(a_ready, i - 1)
                for c in range(KC):
                    last = pe.matmul(ps[:, 2 + b, 0:2 * I], gxT[:, b, c, :],
                                     w13[:, bass.ds(e, 1), :, c, :].rearrange("p a j i -> p (a j) i"),
                                     start=(c == 0), stop=(c == KC - 1))
                last.then_inc(gu_ps, 1)

            def hidden_T(i, b, again):
                pe.wait_ge(a_ready, i + 1)
                if again:
                    pe.wait_ge(aT_ready, i - 1)
                pe.transpose(ps[0:I, 4 + b, 0:P], act_a[:, b, :], ident[:, :]).then_inc(aT_ps, 1)

            def down(i, b, again):
                e = pe.value_load(te_row[0:1, bass.ds(i, 1)], min_val=0, max_val=E - 1)
                pe.wait_ge(aT_ready, i + 1)
                if again:
                    pe.wait_ge(yo_ready, i - 1)
                pe.matmul(ps[:, 6 + b, 0:D], aT[:, b, :], w2s[:, bass.ds(e, 1), :].rearrange("p a d -> p (a d)"),
                          start=True, stop=True).then_inc(y_ps, 1)

            rows_T(0, 0, 0, 16, False)
            rows_T(1, 1, 1, 16, False); gate_up(0, 0, False)
            rows_T(2, 2, 0, 16, True); hidden_T(0, 0, False); gate_up(1, 1, False)
            pe.wait_ge(w2_in, 16 * 8)
            pe.wait_ge(ids_ready, 1)
            rows_T(3, 3, 1, 16, True); hidden_T(1, 1, False); gate_up(2, 0, True); down(0, 0, False)
            rows_T(4, 0, 0, 32, True); hidden_T(2, 0, True); gate_up(3, 1, True); down(1, 1, False)
            rows_T(5, 1, 1, 32, True); hidden_T(3, 1, True); gate_up(4, 0, True); down(2, 0, True)
            rows_T(6, 2, 0, 32, True); hidden_T(4, 0, True); gate_up(5, 1, True); down(3, 1, True)
            rows_T(7, 3, 1, 32, True); hidden_T(5, 1, True); gate_up(6, 0, True); down(4, 0, True)
            with pe.Fori(2, NT // NG) as j:
                for i in range(NG):
                    rows_T(NG * j + i, i, i % 2, 16 * j + 16, True)
                    hidden_T(NG * j + (i - 2), i % 2, True)
                    gate_up(NG * j + (i - 1), 1 - i % 2, True)
                    down(NG * j + (i - 3), 1 - i % 2, True)
            hidden_T(NT - 2, 0, True); gate_up(NT - 1, 1, True); down(NT - 3, 1, True)
            hidden_T(NT - 1, 1, True); down(NT - 2, 0, True)
            down(NT - 1, 1, True)


_INS = ['L0_attn_x', 'L0_attn_Wqkv', 'L0_attn_b_qkv', 'L0_attn_Wout', 'L0_attn_b_out', 'L0_ffn_gate_w', 'L0_ffn_w1',
        'L0_ffn_w3', 'L0_ffn_w2']
_OUTS = [((2, 512, 256), 'float32')]


def kernel(**inputs):
    import numpy as _np
    import concourse.bacc as _bacc
    from concourse import mybir as _mybir
    from concourse.bass_utils import run_bass_kernel_spmd as _run

    nc = _bacc.Bacc("TRN2", target_bir_lowering=False, num_devices=1)
    arrays, args = {}, []
    for name in _INS:
        a = _np.ascontiguousarray(inputs[name])
        arrays[f"in_{name}_dram"] = a
        args.append(nc.dram_tensor(f"in_{name}_dram", a.shape, _mybir.dt.from_np(a.dtype), kind="ExternalInput").ap())
    for i, (shape, dtype) in enumerate(_OUTS):
        dt = _mybir.dt.from_np(_np.dtype(dtype))
        args.append(nc.dram_tensor(f"out_{i}_dram", shape, dt, kind="ExternalOutput").ap())
    layer(nc, *args)
    r = _run(nc, [arrays], core_ids=[0])
    got = tuple(r.results[0][f"out_{i}_dram"] for i in range(len(_OUTS)))
    return got[0]
```

```python
from contextlib import ExitStack

import numpy as np

import concourse.bass as bass
from concourse import mybir

F32 = mybir.dt.float32
BF16 = mybir.dt.bfloat16
F16 = mybir.dt.float16
I32 = mybir.dt.int32
U32 = mybir.dt.uint32
ALU = mybir.AluOpType
ACT = mybir.ActivationFunctionType
AX = mybir.AxisListType

P = 128
NEG = -1.0e30
SLOTS = 3
GR = 4
PRING = 4


def alibi_rows(heads, seq):
    pos = np.arange(1 - seq, 1, dtype=np.float32)
    m = np.arange(1, heads + 1, dtype=np.float32) * np.float32(8.0 / heads)
    slopes = (np.float32(1.0) / np.float32(2.0) ** m).astype(np.float32)
    bias = slopes[:, None] * pos[None, :]
    rows = np.full((6, heads, seq), 0x3F80, dtype=np.uint16)
    for j in range(3):
        top = bias.view(np.uint32) >> 16
        rows[j] = top
        bias = bias - (top << 16).view(np.float32)
    return rows


def layer(nc, x, w_qkv, b_qkv, w_out, b_out, gate_w, w1, w3, w2, out):
    B, S, D = x.shape
    H, HD = 16, D // 16
    E, _, I = w1.shape
    TOPK = 8
    T = B * S // P
    TB = S // P
    KC = D // P
    G = 4
    UNITS = B * H // G
    NT = E + (B * S * TOPK - E) // P + 1
    ROUNDS = NT + GR
    EPS = 1e-5

    x_tiles = x.rearrange("b (t p) d -> p (b t) d", p=P)
    out_tiles = out.rearrange("b (t p) d -> (b t) p d", p=P)

    with ExitStack() as ctx:
        def sem(name):
            return ctx.enter_context(nc.semaphore(name))

        def dram(name, shape, dt):
            return nc.dram_tensor(name, shape, dt, kind="Internal").ap()

        k_rows = nc.inline_tensor(alibi_rows(H, S), "alibi_rows")
        k_rows = (k_rows if isinstance(k_rows, bass.AP) else k_rows.ap()).bitcast(BF16)
        stack_d = dram("stack_d", (B, 4, 8 * HD, 6, S), BF16)
        x1_d = dram("x1_d", (B * S, D), F32)
        y_d = dram("y_d", (NT * P, D), F32)

        def sb(name, shape, dt, c=ctx):
            return c.enter_context(nc.sbuf_tensor(name, shape, dt))

        w13 = sb("w13", [P, E, 2, KC, I], F32)
        X = sb("X", [P, T, D], F32)
        ident = sb("ident", [P, P], F32)
        identb = sb("identb", [P, P], BF16)
        stats = sb("stats", [P, T, 6], F32)
        mv = sb("mv", [P, T, 2], F32)
        rstd = sb("rstd", [P, T], F32)
        gateT = sb("gateT", [P, KC, E], F32)
        att = ExitStack()
        Qs = sb("Qs", [102, 4, G, S], BF16, att)
        Ks = sb("Ks", [102, 4, G, S], BF16, att)
        VH = HD + 1
        V = sb("V", [P, T, H * VH + 16], F32, att)
        WoT = sb("WoT", [P, 4, D], F32, att)
        maskA = sb("maskA", [P, P], BF16, att)
        maskB = sb("maskB", [P, P], BF16, att)
        sumsel = sb("sumsel", [P, G], F32, att)
        pro = ExitStack()
        w_raw = sb("w_raw", [P, 6, D], F32, pro)
        WT = sb("WT", [P, KC, 3 * D], F32, pro)
        xT = sb("xT", [P, KC, B * S], F32, pro)
        qk_f = sb("qk_f", [P, 2, S], F32, pro)
        qk_r = sb("qk_r", [P, 2, S], F32, pro)
        qk_p = sb("qk_p", [P, 2, 3, S], BF16, pro)
        bqk = sb("bqk", [P, 4], F32, pro)
        bv = sb("bv", [P, D], F32, pro)
        bo = sb("bo", [P, D], F32, pro)
        wo_raw = sb("wo_raw", [P, KC, D], F32, pro)
        wo_pad = sb("wo_pad", [P, KC, H * 32], F32, pro)
        gate_raw = sb("gate_raw", [E, D], F32, pro)
        pro.close()
        PT = sb("PT", [P, PRING, 2, S], F32, att)
        ctxT = sb("ctxT", [P, B, 4, S], F32, att)
        OT = sb("OT", [P, S], F32, att)
        rsum = sb("rsum", [P, TB, G], F32, att)
        rsum32 = sb("rsum32", [P, TB, G, 32], F32, att)
        mx = sb("mx", [P, 2, TB, G], F32, att)
        mr = sb("mr", [P, 2, TB, G], F32, att)
        mx3 = sb("mx3", [P, 2, TB, 3, G], BF16, att)
        mT = sb("mT", [3 * G, 2, S], BF16, att)
        att.close()
        w2s = sb("w2s", [I, E, D], F32)
        x1T = sb("x1T", [P, 2, KC, P], F32)
        L = sb("L", [P, T, E], F32)
        Wc = sb("Wc", [P, T, E], F32)
        Sl = sb("Sl", [P, T, E], F32)
        Mk = sb("Mk", [P, T, E], BF16)
        top8 = sb("top8", [P, T, 8], F32)
        sl8 = sb("sl8", [P, T, 8], F32)
        slot_u = sb("slot_u", [P, T, 8], U32)
        slot_i = sb("slot_i", [P, T, 8], I32)
        part_i = sb("part_i", [P, 2, T, 8], I32)
        part_f = sb("part_f", [P, 2, T, 8], F32)
        upper = sb("upper", [P, P], BF16)
        onesb = sb("onesb", [P, P], BF16)
        onesf = sb("onesf", [P, E], F32)
        iota_f = sb("iota_f", [P, P], F32)
        iota_h = sb("iota_h", [P, P], F16)
        tok = sb("tok", [P, T], F32)
        cnt = sb("cnt", [P, 4, E], F32)
        cnt_i = sb("cnt_i", [P, 2, E], I32)
        te = sb("te", [P, E + 1], F32)
        te_row = sb("te_row", [1, ROUNDS], I32)
        ids = sb("ids", [P, ROUNDS], U32)
        zs = sb("zs", [P, 4, T], F32)
        wk = sb("wk", [P, T, 8], F32)
        junk = sb("junk", [P, E], F32)
        ohA = sb("ohA", [P, 4, P], F16)
        ohB = sb("ohB", [P, 4, P], F16)
        NG = 4
        gx = sb("gx", [P, NG, D], F32)
        gxT = sb("gxT", [P, 2, KC, P], F32)
        silu = sb("silu", [P, 2, I], F32)
        act_a = sb("act_a", [P, 2, I], F32)
        aT = sb("aT", [I, 2, P], F32)
        yo = sb("yo", [P, 4, D], F32)

        ps = ctx.enter_context(nc.psum_tensor("ps", [P, 8, 512], F32))

        x_in = [sem(f"x_in{b}") for b in range(B)]
        wqkv_in = sem("wqkv_in"); bias_in = sem("bias_in"); wo_in = sem("wo_in"); rows_in = sem("rows_in")
        consts = sem("consts"); pads = sem("pads")
        pe_job = sem("pe_job"); act_job = sem("act_job"); dve_job = sem("dve_job")
        part1 = sem("part1"); rest1 = sem("rest1"); part2 = sem("part2"); part3 = sem("part3")
        pieces_out = [sem(f"pieces_out{i}") for i in range(2)]
        stack_in = [sem(f"stack_in{i}") for i in range(4)]
        a_done = sem("a_done"); max_done = sem("max_done"); mx3_ready = sem("mx3_ready"); mT_ps = sem("mT_ps")
        mT_ready = sem("mT_ready"); mrow_in = [sem(f"mrow_in{i}") for i in range(4)]
        b_done = sem("b_done"); exp_done = sem("exp_done"); pv_done = sem("pv_done"); ot_ready = sem("ot_ready")
        sums_ps = sem("sums_ps"); rsum_ready = sem("rsum_ready"); rsum32_ready = sem("rsum32_ready"); rows_ps = sem("rows_ps"); ctx_ready = sem("ctx_ready"); proj_ps = sem("proj_ps"); y_ready = sem("y_ready")
        ln_sd = sem("ln_sd"); ln_var = sem("ln_var"); x1_ready = sem("x1_ready"); x1_out = sem("x1_out")
        w13_in = sem("w13_in"); w2_in = sem("w2_in")
        r_xT_ps = sem("r_xT_ps"); r_xT = sem("r_xT"); r_log_ps = sem("r_log_ps"); r_log = sem("r_log")
        mask_ready = sem("mask_ready"); pos_ps = sem("pos_ps"); shifted = sem("shifted"); exps = sem("exps")
        oh_ready = sem("oh_ready"); oh_used = sem("oh_used"); te_ready = sem("te_ready"); te_ps = sem("te_ps")
        te_out = sem("te_out"); ids_ready = sem("ids_ready")
        gx_in = [sem(f"gx_in{i}") for i in range(NG)]
        t_ps = sem("t_ps"); gxT_ready = sem("gxT_ready"); gu_ps = sem("gu_ps"); silu_ready = sem("silu_ready")
        a_ready = sem("a_ready"); aT_ps = sem("aT_ps"); aT_ready = sem("aT_ready"); y_ps = sem("y_ps")
        yo_ready = sem("yo_ready"); y_out = [sem(f"y_out{i}") for i in range(4)]
        row_in = [sem(f"row_in{i}") for i in range(8)]
        wk_ready = sem("wk_ready"); rows_used = sem("rows_used"); fin_ready = sem("fin_ready"); out_done = sem("out_done")
        dve_step = sem("dve_step"); pool_step = sem("pool_step")

        jobs = [("wT", 0), ("wT", 1), ("wT", 2)]
        for b in range(B):
            jobs += [("xT", b, c) for c in range(KC)] + [("qk", b, m) for m in (0, 2, 1, 3)]
        jobs += [("v", t) for t in range(T // 2)] + [("woT", 0), ("woT", 1), ("gT",)]
        on_act = {"wT", "woT", "gT"}
        qk_jobs = [j for j in jobs if j[0] == "qk"]

        def evacuated(eng, i):
            mine = jobs[i][0] in on_act
            n = sum((j[0] in on_act) == mine for j in jobs[:i + 1])
            eng.wait_ge(act_job if mine else dve_job, n)

        uses = []
        for u in range(2):
            uses += [("A", u * 8 + n) for n in range(8)]
        for u in range(UNITS):
            for i in range(TB):
                if u + 2 < UNITS:
                    uses += [("A", (u + 2) * 8 + 2 * i + hp) for hp in range(2)]
                uses += [("B", u * 8 + 2 * i + hp) for hp in range(2)]
        slot_of = {use: n % SLOTS for n, use in enumerate(uses)}

        def slot_free(eng, use):
            n = uses.index(use)
            if n >= SLOTS:
                kind, i = uses[n - SLOTS]
                eng.wait_ge(max_done if kind == "A" else exp_done, i + 1)

        def slot(use):
            return ps[:, 2 * slot_of[use]:2 * slot_of[use] + 2, :]

        def misc_free(eng, kind, i):
            n = misc.index((kind, i))
            if n:
                k, j = misc[n - 1]
                eng.wait_ge({"T": mT_ready, "S": rsum_ready, "L": ctx_ready, "O": y_ready}[k], j + 1)

        misc = [("T", 0)]
        for u in range(UNITS):
            for i in range(TB):
                if i == 0 and u + 1 < UNITS:
                    misc.append(("T", u + 1))
                if i == 2 and u >= 1:
                    misc.append(("S", u - 1))
                if i == 3 and u >= 1:
                    misc.append(("L", u - 1))
                if u == 5:
                    misc.append(("O", i))
        misc += [("S", UNITS - 1), ("L", UNITS - 1)]
        misc += [("O", TB + i) for i in range(TB)]

        block = ctx.enter_context(nc.Block())

        rows = w13[:, 0:8, :, :, :].rearrange("p e j c i -> p e (j c i)")[:, :, 0:D]

        @block.sync
        def _(sp):
            sp.dma_start(w_raw[:, :, :], w_qkv.rearrange("(r p) d -> p r d", p=P)).then_inc(wqkv_in, 16)
            for b in range(B):
                sp.dma_start(X[:, b * TB:(b + 1) * TB, :], x_tiles[:, b * TB:(b + 1) * TB, :]).then_inc(x_in[b], 16)
            sp.dma_start(bqk[:, :], b_qkv[0:2 * D].rearrange("(c p) -> p c", p=P),
                         allow_slow_non_contiguous=True).then_inc(bias_in, 16)
            sp.dma_start(bv[:, :], b_qkv[2 * D:3 * D].partition_broadcast(P)).then_inc(bias_in, 16)
            sp.dma_start(bo[:, :], b_out.partition_broadcast(P)).then_inc(bias_in, 16)
            sp.dma_start(wo_raw[:, :, :], w_out.rearrange("(c p) d -> p c d", p=P)).then_inc(wo_in, 16)
            sp.dma_start(gate_raw[:, :], gate_w).then_inc(wo_in, 16)
            sp.dma_start(Ks[96:102, :, :, :], k_rows.rearrange("r (s g) t -> r s g t", s=4)).then_inc(rows_in, 16)
            sp.dma_start(Qs[96:99, :, :, :], k_rows[3:6].rearrange("r (s g) t -> r s g t", s=4)).then_inc(rows_in, 16)

            def write_pieces(r):
                _, b, m = qk_jobs[r]
                where = (slice(0, 3), slice(3, 5), slice(5, 6)) if m < 2 else (slice(1, 6, 2), slice(0, 5, 4), slice(2, 3))
                for piece, ready in enumerate((part1, part2, part3)):
                    sp.wait_ge(ready, r + 1)
                    dst = stack_d[b, m, :, where[piece], :]
                    sp.dma_start(dst, qk_p[:, r % 2, piece:piece + 1, :].broadcast_to(tuple(dst.shape))
                                 ).then_inc(pieces_out[r % 2], 16)

            def read_stack(u):
                b, g = divmod(u, 4)
                for r in (4 * b + 2 * (g // 2), 4 * b + 2 * (g // 2) + 1):
                    sp.wait_ge(pieces_out[r % 2], 48 * (r // 2 + 1))
                if u >= 4:
                    sp.wait_ge(b_done, (u - 3) * 8)
                h0 = G * (g % 2)
                for dst, m in ((Qs, g // 2), (Ks, 2 + g // 2)):
                    sp.dma_start(dst[0:96, g, :, :],
                                 stack_d[b, m, h0 * HD:(h0 + G) * HD, :, :].rearrange("(h d) j t -> (d j) h t", d=HD)
                                 ).then_inc(stack_in[g], 16)

            def load_w13(n):
                e = slice(4 * n, 4 * n + 4)
                for j, w in enumerate((w1, w3)):
                    sp.dma_start(w13[:, e, j, :, :].rearrange("p e c i -> p e (c i)"),
                                 w[e].rearrange("e (p c) i -> p e (c i)", c=KC)).then_inc(w13_in, 16)

            for r in range(len(qk_jobs)):
                write_pieces(r)
                if r % 2 == 0 and 2 <= r <= 4:
                    read_stack(r - 2)
                    read_stack(r - 1)
            for u in range(4, UNITS):
                for n in range(4):
                    load_w13(4 * (u - 4) + n)
                read_stack(u)
            sp.wait_ge(y_ready, T)
            sp.wait_ge(x1_ready, T)
            for n in range(8):
                sp.dma_start(w2s[:, 8 * n:8 * n + 8, :], w2[8 * n:8 * n + 8].rearrange("e i d -> i e d")).then_inc(w2_in, 16)
            sp.dma_start(x1_d.rearrange("(t p) d -> p t d", p=P), X[:, :, :]).then_inc(x1_out, 16)
            for g in range(1, ROUNDS // GR):
                for t in range(GR * g - 4, GR * g):
                    sp.wait_ge(yo_ready, t + 1)
                    sp.dma_start(y_d[t * P:(t + 1) * P, :], yo[:, t % 4, :]).then_inc(y_out[t % 4], 16)
            for t in range(T):
                sp.wait_ge(fin_ready, t + 1)
                sp.dma_start(out_tiles[t], X[:, t, :]).then_inc(out_done, 16)
            sp.wait_ge(out_done, 16 * T)

        @block.gpsimd
        def _(pool):
            n = 0

            def step(ins):
                nonlocal n
                n += 1
                ins.then_inc(pool_step, 1)
                pool.wait_ge(pool_step, n)

            step(pool.memset(ident[:, :], 1.0))
            step(pool.affine_select(out=ident[:, :], in_=ident[:, :], compare_op=ALU.is_equal, fill=0.0, base=0,
                                    pattern=[[-1, P]], channel_multiplier=1))
            step(pool.memset(wo_pad[:, :, :], 0.0))
            pool.tensor_copy(identb[:, :], ident[:, :]).then_inc(consts, 1)
            step(pool.memset(maskA[:, :], 0.0))
            step(pool.memset(maskB[:, :], 0.0))
            pool.affine_select(out=maskA[:, :], in_=maskA[:, :], compare_op=ALU.is_ge, fill=NEG, base=0,
                               pattern=[[-1, P]], channel_multiplier=1).then_inc(consts, 1)
            pool.affine_select(out=maskB[:, :], in_=maskB[:, :], compare_op=ALU.is_ge, fill=NEG, base=0,
                               pattern=[[1, P]], channel_multiplier=-1).then_inc(consts, 1)
            step(pool.memset(sumsel[:, :], 1.0))
            pool.affine_select(out=sumsel[:, :], in_=sumsel[:, :], compare_op=ALU.is_equal, fill=0.0,
                               base=-HD, pattern=[[-32, G]], channel_multiplier=1).then_inc(consts, 1)
            pool.memset(V[:, :, :], 1.0).then_inc(consts, 1)
            pool.wait_ge(wo_in, 32)
            pool.tensor_copy(wo_pad[:, :, :].rearrange("p c (h d) -> p c h d", d=32)[:, :, :, 0:HD],
                             wo_raw[:, :, :].rearrange("p c (h d) -> p c h d", d=HD)).then_inc(pads, 1)
            for r in range(len(qk_jobs)):
                pool.wait_ge(part2, r + 1)
                if r >= 2:
                    pool.wait_ge(pieces_out[r % 2], 48 * (r // 2))
                pool.tensor_tensor(qk_p[:, r % 2, 2, :], qk_r[:, r % 2, :], qk_p[:, r % 2, 1, :],
                                   ALU.subtract).then_inc(part3, 1)

            def spread(u):
                pool.wait_ge(rsum_ready, u + 1)
                if u:
                    pool.wait_ge(rows_ps, u)
                pool.tensor_copy(rsum32[:, :, :, :], rsum[:, :, :].unsqueeze(3).broadcast_to((P, TB, G, 32))
                                 ).then_inc(rsum32_ready, 1)

            for u in range(UNITS):
                pool.wait_ge(mT_ready, u + 1)
                for j in range(3):
                    pool.dma_start(Qs[99 + j:100 + j, u % 4, :, :], mT[G * j:G * j + G, u % 2, :]).then_inc(mrow_in[u % 4], 16)
                if u >= 2:
                    spread(u - 2)
            spread(UNITS - 2)
            spread(UNITS - 1)
            pool.wait_ge(x1_ready, T)
            step(pool.memset(upper[:, :], 1.0))
            pool.affine_select(out=upper[:, :], in_=upper[:, :], compare_op=ALU.is_gt, fill=0.0, base=0,
                               pattern=[[1, P]], channel_multiplier=-1).then_inc(consts, 1)
            pool.memset(onesb[:, :], 1.0).then_inc(consts, 1)
            pool.memset(onesf[:, :], 1.0).then_inc(consts, 1)
            pool.iota(slot_i[:, :, :].rearrange("p a b -> p (a b)")[:, 0:T], pattern=[[P, T]], base=0,
                      channel_multiplier=1).then_inc(pool_step, 1)
            pool.memset(te_row[:, NT:ROUNDS].bitcast(F32), 0.0).then_inc(consts, 1)
            pool.memset(ids[:, NT:ROUNDS].bitcast(F32), 0.0).then_inc(consts, 1)
            pool.iota(ids[:, 0:NT].bitcast(I32), pattern=[[1, NT]], base=0, channel_multiplier=0).then_inc(pool_step, 1)
            n += 2
            pool.wait_ge(pool_step, n)
            pool.tensor_copy(tok[:, :], slot_i[:, :, :].rearrange("p a b -> p (a b)")[:, 0:T]).then_inc(consts, 1)
            pool.tensor_copy(iota_h[:, :], ids[:, 0:NT].bitcast(I32)).then_inc(consts, 1)
            pool.wait_ge(x1_out, 16)

            pool.wait_ge(ids_ready, 1)
            for i in range(ROUNDS):
                if i >= NG:
                    pool.wait_ge(t_ps, i + 1 - NG)
                pool.indirect_dma_start(gx[:, i % NG, :], None, x1_d,
                                        bass.IndirectOffsetOnAxis(ids[:, i:i + 1], 0)).then_inc(gx_in[i % NG], 16)
            for q in y_out:
                pool.wait_ge(q, 16 * (NT // 4))
            pool.wait_ge(t_ps, NT)
            for n in range(T * TOPK):
                t, k = divmod(n, TOPK)
                if n >= 8:
                    pool.wait_ge(rows_used, n - 7)
                pool.indirect_dma_start(rows[:, n % 8, :], None, y_d,
                                        bass.IndirectOffsetOnAxis(slot_u[:, t, k:k + 1], 0)).then_inc(row_in[n % 8], 16)

        @block.scalar
        def _(act):
            def job(i):
                kind = jobs[i][0]
                bank = ps[:, i % 8, :]
                act.wait_ge(pe_job, i + 1)
                if kind == "wT":
                    g = jobs[i][1]
                    act.copy(WT[:, :, :].rearrange("p c n -> p (c n)")[:, 512 * g:512 * g + 512], bank).then_inc(act_job, 1)
                elif kind == "woT":
                    g = jobs[i][1]
                    act.copy(WoT[:, :, :].rearrange("p g n -> p (g n)")[:, 512 * g:512 * g + 512], bank).then_inc(act_job, 1)
                else:
                    act.copy(gateT[:, :, :].rearrange("p c e -> p (c e)"), bank[:, 0:KC * E]).then_inc(act_job, 1)

            r = 0
            for i, j in enumerate(jobs):
                if j[0] in on_act:
                    job(i)
                elif j[0] == "qk":
                    if r >= 2:
                        act.wait_ge(pieces_out[r % 2], 48 * (r // 2))
                    act.wait_ge(dve_job, sum(q[0] not in on_act for q in jobs[:i + 1]))
                    act.copy(qk_p[:, r % 2, 0, :], qk_f[:, r % 2, :]).then_inc(part1, 1)
                    act.wait_ge(rest1, r + 1)
                    act.copy(qk_p[:, r % 2, 1, :], qk_r[:, r % 2, :]).then_inc(part2, 1)
                    r += 1

            def max_rows(u):
                act.wait_ge(mT_ps, u + 1)
                if u >= 2:
                    act.wait_ge(mrow_in[(u - 2) % 4], 48 * ((u - 2) // 4 + 1))
                act.copy(mT[:, u % 2, :], ps[0:3 * G, 7, :]).then_inc(mT_ready, 1)

            def probs(u, kb, hp):
                n = u * 8 + 2 * kb + hp
                act.wait_ge(b_done, n + 1)
                if n >= PRING:
                    act.wait_ge(pv_done, n - PRING + 1)
                N = S - kb * P
                act.activation(PT[:, n % PRING, :, 0:N], slot(("B", n))[:, :, 0:N], ACT.Exp).then_inc(exp_done, 1)

            def heads_out(u):
                act.wait_ge(pv_done, 8 * (u + 1))
                if u >= 1:
                    act.wait_ge(ctx_ready, u)
                act.copy(OT[:, :], ps[:, 6, :]).then_inc(ot_ready, 1)

            act.wait_ge(pe_job, len(jobs))
            act.wait_ge(part3, len(qk_jobs))
            for q in pieces_out:
                act.wait_ge(q, 48 * len(qk_jobs) // 2)
            max_rows(0)
            for u in range(UNITS):
                if u + 1 < UNITS:
                    max_rows(u + 1)
                for kb in range(TB):
                    for hp in range(2):
                        probs(u, kb, hp)
                    if kb == 0 and u >= 1:
                        heads_out(u - 1)
            heads_out(UNITS - 1)
            act.wait_ge(ln_var, 1)
            act.activation(rstd[:, :], rstd[:, :], ACT.Sqrt).then_inc(ln_sd, 1)
            for t in range(T):
                act.wait_ge(r_xT_ps, t + 1)
                if t >= 2:
                    act.wait_ge(r_log_ps, t - 1)
                act.copy(x1T[:, t % 2, :, :].rearrange("p c n -> p (c n)"), ps[:, t % 2, 0:KC * P]).then_inc(r_xT, 1)
            act.wait_ge(shifted, 1)
            act.activation(Wc[:, :, :], Wc[:, :, :], ACT.Exp).then_inc(exps, 1)
            act.wait_ge(te_ps, 1)
            act.copy(te_row[:, 0:NT], ps[0:1, 6, 0:NT]).then_inc(te_out, 1)
            act.wait_ge(oh_used, T * TOPK)
            act.copy(ids[:, 0:NT], ps[:, 7, 0:NT]).then_inc(ids_ready, 1)

            def round_(i):
                if i >= 1:
                    t = i - 1
                    act.wait_ge(gu_ps, t + 1)
                    act.activation(silu[:, t % 2, :], ps[:, 2 + t % 2, 0:I], ACT.Silu).then_inc(silu_ready, 1)
                if i >= 4:
                    t = i - 4
                    act.wait_ge(y_ps, t + 1)
                    if t >= 4:
                        act.wait_ge(y_out[t % 4], 16 * (t // 4))
                    act.copy(yo[:, t % 4, :], ps[:, 6 + t % 2, 0:D]).then_inc(yo_ready, 1)

            for g in range(ROUNDS // GR):
                for i in range(GR * g, GR * g + GR):
                    round_(i)
            act.wait_ge(ln_var, 2)
            for t in range(T):
                act.wait_ge(ln_var, t + 2)
                act.activation(rstd[:, t:t + 1], rstd[:, t:t + 1], ACT.Sqrt).then_inc(ln_sd, 1)

        @block.vector
        def _(dve):
            n_step = 0

            def step(ins):
                nonlocal n_step
                n_step += 1
                ins.then_inc(dve_step, 1)
                dve.wait_ge(dve_step, n_step)

            def rest(r):
                dve.wait_ge(part1, r + 1)
                if r >= 2:
                    dve.wait_ge(part3, r - 1)
                dve.tensor_tensor(qk_r[:, r % 2, :], qk_f[:, r % 2, :], qk_p[:, r % 2, 0, :],
                                  ALU.subtract).then_inc(rest1, 1)

            dve.wait_ge(bias_in, 48)
            r = 0
            for i, j in enumerate(jobs):
                if j[0] in on_act:
                    continue
                bank = ps[:, i % 8, :]
                dve.wait_ge(pe_job, i + 1)
                if j[0] == "xT":
                    dve.tensor_copy(xT[:, j[2], j[1] * S:(j[1] + 1) * S], bank).then_inc(dve_job, 1)
                elif j[0] == "qk":
                    b, m = j[1:]
                    if r >= 2:
                        dve.wait_ge(rest1, r - 1)
                    dve.tensor_scalar(qk_f[:, r % 2, :], bank, bqk[:, m:m + 1], 0.25 if m < 2 else 1.0,
                                      ALU.add, ALU.mult).then_inc(dve_job, 1)
                    if r >= 1:
                        rest(r - 1)
                    r += 1
                    if r == len(qk_jobs):
                        rest(r - 1)
                elif j[0] == "v":
                    for t in (2 * j[1], 2 * j[1] + 1):
                        if t == 0:
                            dve.wait_ge(consts, 5)
                        ins = dve.tensor_tensor(V[:, t, 0:H * VH].rearrange("p (h d) -> p h d", d=VH)[:, :, 0:HD],
                                                bank[:, (t % 2) * D:(t % 2) * D + D].rearrange("p (h d) -> p h d", d=HD),
                                                bv[:, :].rearrange("p (h d) -> p h d", d=HD), ALU.add)
                    ins.then_inc(dve_job, 1)
            for t in range(T):
                ins = dve.tensor_tensor(X[:, t, :], X[:, t, :], bo[:, :], ALU.add)
            step(ins)

            def row_max(u, i):
                for hp in range(2):
                    n = u * 8 + 2 * i + hp
                    dve.wait_ge(a_done, n + 1)
                    if i == 0 and hp == 0 and u >= 2:
                        dve.wait_ge(mT_ps, u - 1)
                    dve.tensor_reduce(mx[:, u % 2, i, 2 * hp:2 * hp + 2], slot(("A", n))[:, :, 0:(i + 1) * P],
                                      AX.X, ALU.max).then_inc(max_done, 1)

            def max_parts(u):
                m, rr, m3 = mx[:, u % 2], mr[:, u % 2], mx3[:, u % 2]
                dve.wait_ge(max_done, 8 * (u + 1))
                step(dve.tensor_scalar(m3[:, :, 0, :], m, -1.0, None, ALU.mult))
                step(dve.scalar_tensor_tensor(out=rr, in0=m, scalar=-1.0, in1=m3[:, :, 0, :], op0=ALU.mult, op1=ALU.subtract))
                step(dve.tensor_copy(m3[:, :, 1, :], rr))
                dve.tensor_tensor(m3[:, :, 2, :], rr, m3[:, :, 1, :], ALU.subtract).then_inc(mx3_ready, 1)

            def normalise(u):
                b, g = divmod(u, 4)
                dve.wait_ge(rows_ps, u + 1)
                dve.tensor_tensor(ctxT[:, b, g, :], OT[:, :], ps[:, 7, :], ALU.mult).then_inc(ctx_ready, 1)

            def invert(u):
                dve.wait_ge(sums_ps, u + 1)
                if u:
                    dve.wait_ge(rsum32_ready, u)
                dve.reciprocal(rsum[:, :, :].rearrange("p t h -> p (t h)"), ps[:, 7, 0:TB * G]).then_inc(rsum_ready, 1)

            def residual(t):
                dve.wait_ge(proj_ps, t + 1)
                dve.tensor_tensor(X[:, t, :], ps[:, 7, 0:D], X[:, t, :], ALU.add).then_inc(y_ready, 1)

            dve.wait_ge(pe_job, len(jobs))
            dve.wait_ge(act_job, sum(j[0] in on_act for j in jobs))
            dve.wait_ge(part3, len(qk_jobs))
            for q in pieces_out:
                dve.wait_ge(q, 48 * len(qk_jobs) // 2)
            for u in range(2):
                for i in range(TB):
                    row_max(u, i)
                max_parts(u)
            for u in range(UNITS):
                for i in range(TB):
                    if u + 2 < UNITS:
                        row_max(u + 2, i)
                    if i == 2 and u >= 1:
                        invert(u - 1)
                    if i == 3 and u >= 1:
                        normalise(u - 1)
                    if u == 5:
                        residual(i)
                if u + 2 < UNITS:
                    max_parts(u + 2)
            invert(UNITS - 1)
            normalise(UNITS - 1)
            for i in range(TB):
                residual(TB + i)

            def statistics(t):
                step(dve.bn_stats(stats[:, t, :], X[:, t, :]))
                dve.bn_aggr(mv[:, t, :], stats[:, t, :])

            dve.wait_ge(y_ready, T)
            for t in range(T):
                step(dve.bn_stats(stats[:, t, :], X[:, t, :]))
            for t in range(T):
                ins = dve.bn_aggr(mv[:, t, :], stats[:, t, :])
            step(ins)
            dve.tensor_scalar(rstd[:, :], mv[:, :, 1], EPS, None, ALU.add).then_inc(ln_var, 1)
            dve.wait_ge(ln_sd, 1)
            step(dve.reciprocal(rstd[:, :], rstd[:, :]))
            for t in range(T):
                dve.tensor_scalar(X[:, t, :], X[:, t, :], mv[:, t, 0:1], rstd[:, t:t + 1],
                                  ALU.subtract, ALU.mult).then_inc(x1_ready, 1)
            for t in range(T):
                dve.wait_ge(r_log_ps, t + 1)
                step(dve.tensor_copy(L[:, t, :], ps[:, 2 + t % 2, 0:E]))
                step(dve.max(top8[:, t, :], L[:, t, :]))
                dve.match_replace(out=Sl[:, t, :], in_to_replace=top8[:, t, :], in_values=L[:, t, :],
                                  imm_value=-3.0e38).then_inc(r_log, 1)
            dve.wait_ge(r_log, T)
            dve.tensor_tensor(Mk[:, :, :], Sl[:, :, :], L[:, :, :], ALU.not_equal).then_inc(mask_ready, 1)
            dve.tensor_tensor(Wc[:, :, :], L[:, :, :], top8[:, :, 0:1].broadcast_to((P, T, E)), ALU.subtract).then_inc(shifted, 1)
            dve.wait_ge(pos_ps, 2)
            step(dve.tensor_scalar(cnt_i[:, 0, :], ps[:, 5, 0:E], float(P - 1), None, ALU.add))
            step(dve.tensor_scalar(cnt_i[:, 1, :], cnt_i[:, 0, :], 7, None, ALU.logical_shift_right))
            step(dve.tensor_copy(cnt[:, 0, :], cnt_i[:, 1, :]))
            dve.wait_ge(consts, 12)
            step(dve.tensor_tensor_scan(cnt[:, 1, :], onesf[:, :], cnt[:, 0, :], 0.0, ALU.mult, ALU.add))
            step(dve.tensor_tensor(cnt[:, 2, :], cnt[:, 1, :], cnt[:, 0, :], ALU.subtract))
            step(dve.tensor_scalar(cnt[:, 3, :], cnt[:, 2, :], float(P), 1.0, ALU.mult, ALU.add))
            step(dve.tensor_scalar(te[:, 0:E], cnt[:, 1, :], tok[:, 0:1], None, ALU.is_le))
            step(dve.tensor_reduce(te[:, E:E + 1], te[:, 0:E], AX.X, ALU.add))
            dve.tensor_scalar(te[:, 0:1], te[:, E:E + 1], float(E - 1), None, ALU.min).then_inc(te_ready, 1)
            step(dve.tensor_tensor(Sl[:, :, :], ps[:, 4, :].rearrange("p (t e) -> p t e", e=E),
                                   cnt[:, 3:4, :].broadcast_to((P, T, E)), ALU.add))
            step(dve.tensor_tensor(Sl[:, :, :], Sl[:, :, :], Mk[:, :, :], ALU.mult))
            for t in range(T):
                ins = dve.max(sl8[:, t, :], Sl[:, t, :])
            step(ins)
            step(dve.tensor_scalar(slot_i[:, :, :], sl8[:, :, :], -1.0, None, ALU.add))
            dve.tensor_copy(slot_u[:, :, :], slot_i[:, :, :])
            dve.tensor_scalar(part_i[:, 0], slot_i[:, :, :], P - 1, None, ALU.bitwise_and)
            step(dve.tensor_scalar(part_i[:, 1], slot_i[:, :, :], 7, None, ALU.logical_shift_right))
            step(dve.tensor_copy(part_f[:, :, :, :], part_i[:, :, :, :]))
            for n in range(T * TOPK):
                t, k = divmod(n, TOPK)
                if n >= 4:
                    dve.wait_ge(oh_used, n - 3)
                dve.tensor_scalar(ohA[:, n % 4, :], iota_h[:, :], part_f[:, 0, t, k:k + 1], None, ALU.is_equal)
                dve.tensor_scalar(ohB[:, n % 4, :], iota_h[:, :], part_f[:, 1, t, k:k + 1], tok[:, t:t + 1],
                                  ALU.is_equal, ALU.mult).then_inc(oh_ready, 1)
            dve.wait_ge(exps, 1)
            step(dve.tensor_reduce(zs[:, 0, :], Wc[:, :, :], AX.X, ALU.add))
            step(dve.tensor_tensor(Wc[:, :, :], Wc[:, :, :], Mk[:, :, :], ALU.mult))
            step(dve.tensor_reduce(zs[:, 1, :], Wc[:, :, :], AX.X, ALU.add))
            step(dve.scalar_tensor_tensor(out=zs[:, 2, :], in0=zs[:, 0, :], scalar=1e-20, in1=zs[:, 1, :],
                                          op0=ALU.mult, op1=ALU.add))
            step(dve.reciprocal(zs[:, 3, :], zs[:, 2, :]))
            for t in range(T):
                ins = dve.tensor_scalar(Wc[:, t, :], Wc[:, t, :], zs[:, 3, t:t + 1], None, ALU.mult)
            step(ins)

            def round_(i):
                dve.wait_ge(t_ps, i + 1)
                dve.tensor_copy(gxT[:, i % 2, :, :].rearrange("p c n -> p (c n)"), ps[:, i % 2, 0:KC * P]).then_inc(gxT_ready, 1)
                if i >= 3:
                    t = i - 3
                    dve.wait_ge(aT_ps, t + 1)
                    if t >= 2:
                        dve.wait_ge(y_ps, t - 1)
                    dve.tensor_copy(aT[:, t % 2, :], ps[0:I, 4 + t % 2, 0:P]).then_inc(aT_ready, 1)
                if i >= 1:
                    t = i - 1
                    dve.wait_ge(silu_ready, t + 1)
                    dve.tensor_tensor(act_a[:, t % 2, :], silu[:, t % 2, :], ps[:, 2 + t % 2, I:2 * I],
                                      ALU.mult).then_inc(a_ready, 1)

            for g in range(ROUNDS // GR):
                for i in range(GR * g, GR * g + GR):
                    round_(i)

            for t in range(T):
                for k in range(TOPK):
                    if k or t:
                        dve.wait_ge(wk_ready, t * TOPK + k)
                    dve.scalar_tensor_tensor(out=junk[:, :], in0=Sl[:, t, :], scalar=sl8[:, t, k:k + 1], in1=Wc[:, t, :],
                                             op0=ALU.is_equal, op1=ALU.mult, accum_out=wk[:, t, k:k + 1]).then_inc(wk_ready, 1)
            dve.wait_ge(wk_ready, T * TOPK)
            for t in range(T):
                for k in range(TOPK):
                    n = t * TOPK + k
                    dve.wait_ge(row_in[n % 8], 16 * (n // 8 + 1))
                    if n:
                        dve.wait_ge(rows_used, n)
                    dve.scalar_tensor_tensor(out=X[:, t, :], in0=rows[:, n % 8, :], scalar=wk[:, t, k:k + 1], in1=X[:, t, :],
                                             op0=ALU.mult, op1=ALU.add).then_inc(rows_used, 1)
                dve.wait_ge(rows_used, (t + 1) * TOPK)
                step(dve.bn_stats(stats[:, t, :], X[:, t, :]))
                step(dve.bn_aggr(mv[:, t, :], stats[:, t, :]))
                dve.tensor_scalar(rstd[:, t:t + 1], mv[:, t, 1:2], EPS, None, ALU.add).then_inc(ln_var, 1)
                dve.wait_ge(ln_sd, t + 2)
                step(dve.reciprocal(rstd[:, t:t + 1], rstd[:, t:t + 1]))
                dve.tensor_scalar(X[:, t, :], X[:, t, :], mv[:, t, 0:1], rstd[:, t:t + 1],
                                  ALU.subtract, ALU.mult).then_inc(fin_ready, 1)

        @block.tensor
        def _(pe):
            pe.wait_ge(consts, 1)
            pe.wait_ge(wqkv_in, 16)
            for i, j in enumerate(jobs):
                kind, bank = j[0], ps[:, i % 8, :]
                if i >= 8:
                    evacuated(pe, i - 8)
                if kind == "wT":
                    for n in range(4):
                        c, r = divmod(4 * j[1] + n, 6)
                        last = pe.transpose(bank[:, n * P:(n + 1) * P], w_raw[:, r, c * P:(c + 1) * P], ident[:, :])
                elif kind == "xT":
                    b, c = j[1:]
                    pe.wait_ge(x_in[b], 16)
                    for t in range(TB):
                        last = pe.transpose(bank[:, t * P:(t + 1) * P], X[:, b * TB + t, c * P:(c + 1) * P], ident[:, :])
                elif kind == "qk":
                    b, m = j[1:]
                    if m == 0:
                        evacuated(pe, 2)
                        evacuated(pe, jobs.index(("xT", b, KC - 1)))
                    for c in range(KC):
                        last = pe.matmul(bank, WT[:, c, m * P:(m + 1) * P], xT[:, c, b * S:(b + 1) * S],
                                         start=(c == 0), stop=(c == KC - 1))
                elif kind == "v":
                    for t in (2 * j[1], 2 * j[1] + 1):
                        for c in range(KC):
                            last = pe.matmul(bank[:, (t % 2) * D:(t % 2) * D + D], xT[:, c, t * P:(t + 1) * P],
                                             WT[:, c, 2 * D:3 * D], start=(c == 0), stop=(c == KC - 1))
                elif kind == "woT":
                    pe.wait_ge(pads, 1)
                    for n in range(4):
                        g, c = divmod(4 * j[1] + n, KC)
                        last = pe.transpose(bank[:, n * P:(n + 1) * P], wo_pad[:, c, g * P:(g + 1) * P], ident[:, :])
                else:
                    for c in range(KC):
                        last = pe.transpose(bank[:, c * E:(c + 1) * E], gate_raw[:, c * P:(c + 1) * P], ident[0:E, 0:E])
                last.then_inc(pe_job, 1)
            for i in range(len(jobs) - 8, len(jobs)):
                evacuated(pe, i)
            pe.wait_ge(consts, 5)
            pe.wait_ge(rows_in, 32)

            def scores_A(u, i):
                s = u % 4
                if i == 0:
                    pe.wait_ge(stack_in[s], 32 * (u // 4 + 1))
                for hp in range(2):
                    n = u * 8 + 2 * i + hp
                    slot_free(pe, ("A", n))
                    dst = slot(("A", n))
                    for j in range(2):
                        h = 2 * hp + j
                        pe.matmul(dst[:, j, 0:(i + 1) * P], Qs[0:99, s, h, i * P:(i + 1) * P], Ks[0:99, s, h, 0:(i + 1) * P],
                                  start=True, stop=False)
                        last = pe.matmul(dst[:, j, i * P:(i + 1) * P], identb[:, :], maskA[:, :], start=False, stop=True)
                    last.then_inc(a_done, 1)

            def scores_B(u, kb):
                s = u % 4
                if kb == 0:
                    pe.wait_ge(mrow_in[s], 48 * (u // 4 + 1))
                for hp in range(2):
                    n = u * 8 + 2 * kb + hp
                    slot_free(pe, ("B", n))
                    dst = slot(("B", n))
                    for j in range(2):
                        h = 2 * hp + j
                        pe.matmul(dst[:, j, 0:S - kb * P], Ks[:, s, h, kb * P:(kb + 1) * P], Qs[:, s, h, kb * P:S],
                                  start=True, stop=False)
                        last = pe.matmul(dst[:, j, 0:P], identb[:, :], maskB[:, :], start=False, stop=True)
                    last.then_inc(b_done, 1)

            def values(u, kb):
                b, g = divmod(u, 4)
                if kb == 0 and u:
                    pe.wait_ge(ot_ready, u)
                for hp in range(2):
                    n = u * 8 + 2 * kb + hp
                    pe.wait_ge(exp_done, n + 1)
                    for j in range(2):
                        h = 2 * hp + j
                        last = pe.matmul(ps[32 * h:32 * h + 32, 6, kb * P:S],
                                         V[:, b * TB + kb, (G * g + h) * VH:(G * g + h) * VH + 32],
                                         PT[:, n % PRING, j, 0:S - kb * P], start=(kb == 0), stop=(kb == TB - 1))
                    last.then_inc(pv_done, 1)

            def max_rows(u):
                pe.wait_ge(mx3_ready, u + 1)
                misc_free(pe, "T", u)
                for i in range(TB):
                    last = pe.matmul(ps[0:3 * G, 7, i * P:(i + 1) * P],
                                     mx3[:, u % 2, i, :, :].rearrange("p j h -> p (j h)"), identb[:, :], start=True, stop=True)
                last.then_inc(mT_ps, 1)

            def sums(u):
                pe.wait_ge(ot_ready, u + 1)
                misc_free(pe, "S", u)
                for i in range(TB):
                    last = pe.matmul(ps[:, 7, G * i:G * i + G], OT[:, i * P:(i + 1) * P], sumsel[:, :], start=True, stop=True)
                last.then_inc(sums_ps, 1)

            def factors(u):
                pe.wait_ge(rsum32_ready, u + 1)
                misc_free(pe, "L", u)
                for i in range(TB):
                    last = pe.transpose(ps[:, 7, i * P:(i + 1) * P], rsum32[:, i, :, :].rearrange("p h r -> p (h r)"), ident[:, :])
                last.then_inc(rows_ps, 1)

            def project(t):
                b = t // TB
                pe.wait_ge(ctx_ready, 4 * (b + 1))
                misc_free(pe, "O", t)
                for g in range(4):
                    last = pe.matmul(ps[:, 7, 0:D], ctxT[:, b, g, (t % TB) * P:(t % TB + 1) * P], WoT[:, g, :],
                                     start=(g == 0), stop=(g == 3))
                last.then_inc(proj_ps, 1)

            for i in range(TB):
                scores_A(0, i)
            for i in range(TB):
                scores_A(1, i)
            max_rows(0)
            for u in range(UNITS):
                for i in range(TB):
                    if i == 0 and u + 1 < UNITS:
                        max_rows(u + 1)
                    if u + 2 < UNITS:
                        scores_A(u + 2, i)
                    scores_B(u, i)
                    if i:
                        values(u, i - 1)
                    if i == 2 and u >= 1:
                        sums(u - 1)
                    if i == 3 and u >= 1:
                        factors(u - 1)
                    if u == 5:
                        project(i)
                values(u, TB - 1)
            sums(UNITS - 1)
            factors(UNITS - 1)
            for i in range(TB):
                project(TB + i)

            pe.wait_ge(y_ready, T)
            for t in range(T):
                pe.wait_ge(x1_ready, t + 1)
                if t >= 2:
                    pe.wait_ge(r_xT, t - 1)
                for c in range(KC):
                    last = pe.transpose(ps[:, t % 2, c * P:(c + 1) * P], X[:, t, c * P:(c + 1) * P], ident[:, :])
                last.then_inc(r_xT_ps, 1)
                pe.wait_ge(r_xT, t + 1)
                if t >= 2:
                    pe.wait_ge(r_log, t - 1)
                for c in range(KC):
                    last = pe.matmul(ps[:, 2 + t % 2, 0:E], x1T[:, t % 2, c, :], gateT[:, c, :], start=(c == 0), stop=(c == KC - 1))
                last.then_inc(r_log_ps, 1)
            pe.wait_ge(consts, 12)
            pe.wait_ge(mask_ready, 1)
            for t in range(T):
                for q in range(t + 1):
                    last = pe.matmul(ps[:, 4, t * E:(t + 1) * E], upper[:, :] if q == t else onesb[:, :], Mk[:, q, :],
                                     start=(q == 0), stop=(q == t))
            last.then_inc(pos_ps, 1)
            for q in range(T):
                last = pe.matmul(ps[:, 5, 0:E], onesb[:, :], Mk[:, q, :], start=(q == 0), stop=(q == T - 1))
            last.then_inc(pos_ps, 1)
            pe.wait_ge(te_ready, 1)
            pe.matmul(ps[0:1, 6, 0:NT], te[:, 0:1], ident[:, :], start=True, stop=True).then_inc(te_ps, 1)
            for n in range(T * TOPK):
                pe.wait_ge(oh_ready, n + 1)
                pe.matmul(ps[:, 7, 0:NT], ohA[:, n % 4, :], ohB[:, n % 4, :], start=(n == 0),
                          stop=(n == T * TOPK - 1)).then_inc(oh_used, 1)
            pe.wait_ge(te_out, 1)
            pe.wait_ge(w13_in, 16 * 2 * E // 4)

            e = {}

            def round_(i):
                pe.wait_ge(gx_in[i % NG], 16 * (i // NG + 1))
                v = gx[:, i % NG, :].rearrange("p (n c) -> p c n", c=KC)
                for c in range(KC):
                    last = pe.transpose(ps[:, i % 2, c * P:(c + 1) * P], v[:, c, :], ident[:, :])
                last.then_inc(t_ps, 1)
                e[i] = pe.value_load(te_row[0:1, i:i + 1], min_val=0, max_val=E - 1)
                if i >= 3:
                    t = i - 3
                    pe.wait_ge(a_ready, t + 1)
                    pe.transpose(ps[0:I, 4 + t % 2, 0:P], act_a[:, t % 2, :], ident[:, :]).then_inc(aT_ps, 1)
                if i >= 1:
                    t = i - 1
                    pe.wait_ge(gxT_ready, t + 1)
                    for c in range(KC):
                        last = pe.matmul(ps[:, 2 + t % 2, 0:2 * I], gxT[:, t % 2, c, :],
                                         w13[:, bass.ds(e[t], 1), :, c, :].rearrange("p a j i -> p (a j) i"),
                                         start=(c == 0), stop=(c == KC - 1))
                    last.then_inc(gu_ps, 1)
                if i >= 4:
                    t = i - 4
                    pe.wait_ge(aT_ready, t + 1)
                    if t >= 2:
                        pe.wait_ge(yo_ready, t - 1)
                    else:
                        pe.wait_ge(w2_in, 16 * 8)
                    pe.matmul(ps[:, 6 + t % 2, 0:D], aT[:, t % 2, :], w2s[:, bass.ds(e.pop(t), 1), :].rearrange("p a d -> p (a d)"),
                              start=True, stop=True).then_inc(y_ps, 1)

            for g in range(ROUNDS // GR):
                for i in range(GR * g, GR * g + GR):
                    round_(i)


_INS = ['L0_attn_x', 'L0_attn_Wqkv', 'L0_attn_b_qkv', 'L0_attn_Wout', 'L0_attn_b_out', 'L0_ffn_gate_w', 'L0_ffn_w1',
        'L0_ffn_w3', 'L0_ffn_w2']
_OUTS = [((2, 512, 256), 'float32')]


def kernel(**inputs):
    import numpy as _np
    import concourse.bacc as _bacc
    from concourse import mybir as _mybir
    from concourse.bass_utils import run_bass_kernel_spmd as _run

    nc = _bacc.Bacc("TRN2", target_bir_lowering=False, num_devices=1)
    arrays, args = {}, []
    for name in _INS:
        a = _np.ascontiguousarray(inputs[name])
        arrays[f"in_{name}_dram"] = a
        args.append(nc.dram_tensor(f"in_{name}_dram", a.shape, _mybir.dt.from_np(a.dtype), kind="ExternalInput").ap())
    for i, (shape, dtype) in enumerate(_OUTS):
        dt = _mybir.dt.from_np(_np.dtype(dtype))
        args.append(nc.dram_tensor(f"out_{i}_dram", shape, dt, kind="ExternalOutput").ap())
    layer(nc, *args)
    r = _run(nc, [arrays], core_ids=[0])
    got = tuple(r.results[0][f"out_{i}_dram"] for i in range(len(_OUTS)))
    return got[0]
```

```python
from contextlib import ExitStack

import numpy as np

import concourse.bass as bass
from concourse import mybir

F32 = mybir.dt.float32
BF16 = mybir.dt.bfloat16
F16 = mybir.dt.float16
I32 = mybir.dt.int32
U32 = mybir.dt.uint32
ALU = mybir.AluOpType
ACT = mybir.ActivationFunctionType
AX = mybir.AxisListType

P = 128
NEG = -1.0e30
SLOTS = 3
GR = 4
PRING = 4
NQ = 4


def alibi_rows(heads, seq):
    pos = np.arange(1 - seq, 1, dtype=np.float32)
    m = np.arange(1, heads + 1, dtype=np.float32) * np.float32(8.0 / heads)
    slopes = (np.float32(1.0) / np.float32(2.0) ** m).astype(np.float32)
    bias = slopes[:, None] * pos[None, :]
    rows = np.full((6, heads, seq), 0x3F80, dtype=np.uint16)
    for j in range(3):
        top = bias.view(np.uint32) >> 16
        rows[j] = top
        bias = bias - (top << 16).view(np.float32)
    return rows


def layer(nc, x, w_qkv, b_qkv, w_out, b_out, gate_w, w1, w3, w2, out):
    B, S, D = x.shape
    H, HD = 16, D // 16
    E, _, I = w1.shape
    TOPK = 8
    T = B * S // P
    TB = S // P
    KC = D // P
    G = 4
    UNITS = B * H // G
    NT = E + (B * S * TOPK - E) // P + 1
    ROUNDS = NT + GR
    SURE = B * S * TOPK // P
    EPS = 1e-5

    x_tiles = x.rearrange("b (t p) d -> p (b t) d", p=P)
    out_tiles = out.rearrange("b (t p) d -> (b t) p d", p=P)

    with ExitStack() as ctx:
        def sem(name):
            return ctx.enter_context(nc.semaphore(name))

        def dram(name, shape, dt):
            return nc.dram_tensor(name, shape, dt, kind="Internal").ap()

        k_rows = nc.inline_tensor(alibi_rows(H, S), "alibi_rows")
        k_rows = (k_rows if isinstance(k_rows, bass.AP) else k_rows.ap()).bitcast(BF16)
        parts_d = dram("parts_d", (B, 4, 3, HD, 8, S), BF16)
        x1_d = dram("x1_d", (B * S, D), F32)
        y_d = dram("y_d", (NT * P, D), F32)

        def sb(name, shape, dt, c=ctx):
            return c.enter_context(nc.sbuf_tensor(name, shape, dt))

        w13 = sb("w13", [P, E, 2, KC, I], F32)
        X = sb("X", [P, T, D], F32)
        ident = sb("ident", [P, P], F32)
        identb = sb("identb", [P, P], BF16)
        stats = sb("stats", [P, T, 6], F32)
        mv = sb("mv", [P, T, 2], F32)
        rstd = sb("rstd", [P, T], F32)
        gateT = sb("gateT", [P, KC, E], F32)
        x1T = sb("x1T", [P, 4, KC, P], F32)
        L = sb("L", [P, T, E], F32)
        Sl = sb("Sl", [P, T, E], F32)
        Mk = sb("Mk", [P, T, E], BF16)
        top8 = sb("top8", [P, T, 8], F32)
        upper = sb("upper", [P, P], BF16)
        onesb = sb("onesb", [P, P], BF16)
        onesf = sb("onesf", [P, E], F32)
        tok_i = sb("tok_i", [P, T], I32)
        tok = sb("tok", [P, T], F32)
        te_row = sb("te_row", [1, ROUNDS], I32)
        used_i = sb("used_i", [1, 1], I32)
        ids = sb("ids", [P, ROUNDS], U32)
        att = ExitStack()
        Qs = sb("Qs", [102, 4, G, S], BF16, att)
        Ks = sb("Ks", [102, 4, G, S], BF16, att)
        VH = HD + 1
        V = sb("V", [P, T, H * VH + 16], F32, att)
        WoT = sb("WoT", [P, 4, D], F32, att)
        maskA = sb("maskA", [P, P], BF16, att)
        maskB = sb("maskB", [P, P], BF16, att)
        bo = sb("bo", [P, 1, D], F32, att)
        zero = bo
        mx = sb("mx", [P, 2, TB, G], F32, att)
        mr = sb("mr", [P, 2, TB, G], F32, att)
        mx3 = sb("mx3", [P, 2, TB, 3, G], BF16, att)
        pro = ExitStack()
        w_raw = sb("w_raw", [P, 6, D], F32, pro)
        WT = sb("WT", [P, KC, 3 * D], F32, pro)
        xT = sb("xT", [P, KC, B * S], F32, pro)
        qk_f = sb("qk_f", [P, 2, S], F32, pro)
        qk_r = sb("qk_r", [P, 2, S], F32, pro)
        qk_p = sb("qk_p", [P, NQ, 3, S], BF16, pro)
        bqk = sb("bqk", [P, 4], F32, pro)
        wo_pad = w13[:, E - 3:E, :, :, :].rearrange("p e j c i -> p (e j c i)")[:, 0:KC * H * 32].rearrange(
            "p (c n) -> p c n", c=KC)
        bv = Sl[:, 0:D // E, :].rearrange("p a b -> p (a b)")
        wo_raw = L[:, :, :].rearrange("p a b -> p (a b)").rearrange("p (c d) -> p c d", c=KC)
        gate_raw = x1T[0:E, 0, :, :].rearrange("p a b -> p (a b)")
        pro.close()
        PT = sb("PT", [P, PRING, 2, S], F32, att)
        ctxT = sb("ctxT", [P, B, 4, S], F32, att)
        OT = sb("OT", [P, 2, S], F32, att)
        OB = sb("OB", [P, S], F32, att)
        factor = sb("factor", [P, 2, S], F32, att)
        rsum = sb("rsum", [P, S // 32], F32, att)
        mT = sb("mT", [3 * G, 2, S], BF16, att)
        att.close()
        w2s = sb("w2s", [I, E, D], F32)
        Wc = sb("Wc", [P, T, E], F32)
        sl8 = sb("sl8", [P, T, 8], F32)
        slot_u = sb("slot_u", [P, T, 8], U32)
        slot_i = sb("slot_i", [P, T, 8], I32)
        part_i = sb("part_i", [P, 2, T, 8], I32)
        part_h = sb("part_h", [P, 2, T, 8], F16)
        cnt = sb("cnt", [P, 4, E], F32)
        cnt_i = sb("cnt_i", [P, 2, E], I32)
        te = sb("te", [P, E + 1], F32)
        zs = sb("zs", [P, 4, T], F32)
        wk = sb("wk", [P, T, 8], F32)
        junk = sb("junk", [P, 4, E], F32)
        onehots = ExitStack()
        iota_i = sb("iota_i", [P, P * 8], I32, onehots)
        iota_h = sb("iota_h", [P, P, 8], F16, onehots)
        ohA = sb("ohA", [P, 2, P, 8], F16, onehots)
        ohB = sb("ohB", [P, 2, P, 8], F16, onehots)
        ohBt = sb("ohBt", [P, 2, P, 8], F16, onehots)
        onehots.close()
        NG = 4
        gx = sb("gx", [P, NG, D], F32)
        gxT = sb("gxT", [P, 2, KC, P], F32)
        silu = sb("silu", [P, 2, I], F32)
        act_a = sb("act_a", [P, 2, I], F32)
        aT = sb("aT", [I, 2, P], F32)
        yo = sb("yo", [P, 4, D], F32)

        ps = ctx.enter_context(nc.psum_tensor("ps", [P, 8, 512], F32))

        x_in = [sem(f"x_in{b}") for b in range(B)]
        wqkv_in = sem("wqkv_in"); bias_in = sem("bias_in"); wo_in = sem("wo_in"); rows_in = sem("rows_in")
        consts = sem("consts"); pads = sem("pads")
        pe_job = sem("pe_job"); act_job = sem("act_job"); dve_job = sem("dve_job")
        part1 = sem("part1"); rest1 = sem("rest1"); part2 = sem("part2"); part3 = sem("part3")
        pieces_out = [sem(f"pieces_out{i}") for i in range(NQ)]
        third_out = [sem(f"third_out{i}") for i in range(NQ)]
        stack_in = [sem(f"stack_in{i}") for i in range(4)]
        a_done = sem("a_done"); max_done = sem("max_done"); mx3_ready = sem("mx3_ready"); mT_ps = sem("mT_ps")
        mT_ready = sem("mT_ready"); mrow_in = [sem(f"mrow_in{i}") for i in range(4)]
        b_done = sem("b_done"); exp_done = sem("exp_done"); pv_done = sem("pv_done"); ot_ready = sem("ot_ready")
        factor_ready = sem("factor_ready"); last_ctx = sem("last_ctx"); ctx_ready = sem("ctx_ready"); proj_ps = sem("proj_ps"); y_ready = sem("y_ready")
        ln_sd = sem("ln_sd"); ln_var = sem("ln_var"); x1_ready = sem("x1_ready"); x1_out = sem("x1_out")
        w13_in = sem("w13_in"); w2_in = sem("w2_in")
        r_xT_ps = sem("r_xT_ps"); r_xT = sem("r_xT"); r_log_ps = sem("r_log_ps"); r_log = sem("r_log")
        mask_ready = sem("mask_ready"); pos_ps = sem("pos_ps"); shifted = sem("shifted"); exps = sem("exps")
        xb_ready = sem("xb_ready"); ohBt_ready = sem("ohBt_ready"); ohA_ready = sem("ohA_ready"); ohB_ready = sem("ohB_ready"); oh_used = sem("oh_used"); te_ready = sem("te_ready"); te_ps = sem("te_ps")
        te_out = sem("te_out"); used_ready = sem("used_ready"); zero_ready = sem("zero_ready"); zero_out = sem("zero_out"); tiles_out = sem("tiles_out"); tiles_done = sem("tiles_done"); ids_ready = sem("ids_ready")
        gx_in = [sem(f"gx_in{i}") for i in range(NG)]
        t_ps = sem("t_ps"); gxT_ready = sem("gxT_ready"); gu_ps = sem("gu_ps"); silu_ready = sem("silu_ready")
        a_ready = sem("a_ready"); aT_ps = sem("aT_ps"); aT_ready = sem("aT_ready"); y_ps = sem("y_ps")
        yo_ready = sem("yo_ready"); y_out = [sem(f"y_out{i}") for i in range(4)]
        row_in = [sem(f"row_in{i}") for i in range(8)]
        wk_ready = sem("wk_ready"); rows_used = sem("rows_used"); fin_ready = sem("fin_ready"); out_done = sem("out_done")
        dve_step = sem("dve_step"); pool_step = sem("pool_step")

        jobs = [("wT", 0), ("wT", 1), ("wT", 2)]
        for b in range(B):
            jobs += [("xT", b, c) for c in range(KC)] + [("qk", b, m) for m in (0, 2, 1, 3)]
        jobs += [("v", t) for t in range(T // 2)] + [("woT", 0), ("woT", 1), ("gT",)]
        on_act = {"wT", "woT", "gT"}
        qk_jobs = [j for j in jobs if j[0] == "qk"]

        def evacuated(eng, i):
            mine = jobs[i][0] in on_act
            n = sum((j[0] in on_act) == mine for j in jobs[:i + 1])
            eng.wait_ge(act_job if mine else dve_job, n)

        uses = [("A", n) for n in range(16)]
        for u in range(UNITS):
            for n in range(8):
                uses.append(("B", u * 8 + n))
                if u + 2 < UNITS:
                    uses.append(("A", (u + 2) * 8 + n))
        both = len(uses) - 16
        slot_of = {use: n % SLOTS if n < both else n % 2 for n, use in enumerate(uses)}

        def slot_read(eng, use):
            kind, i = use
            eng.wait_ge(max_done if kind == "A" else exp_done, i + 1)

        def slot_free(eng, use):
            before = [v for v in uses[:uses.index(use)] if slot_of[v] == slot_of[use]]
            if before:
                slot_read(eng, before[-1])

        def slot(use):
            return ps[:, 2 * slot_of[use]:2 * slot_of[use] + 2, :]

        def pair_end(t):
            return t - t % 2 + 2

        def router_bank(t):
            return ps[:, 7, t % 2 * 256:t % 2 * 256 + 256] if t < TB else ps[:, 2 + t % TB, 0:256]

        def proj_bank(t):
            bank = 7 if t < TB else 4 + (t - TB) // 2
            return ps[:, bank, t % 2 * D:t % 2 * D + D]

        def expert_rounds(eng, group):
            eng.wait_ge(used_ready, 1)
            used = eng.value_load(used_i[0:1, 0:1], min_val=SURE, max_val=NT - 1)
            with ExitStack() as nest:
                for g in range(ROUNDS // GR):
                    if g > SURE // GR:
                        nest.enter_context(eng.If(used > GR * (g - 1)))
                    group(g)

        block = ctx.enter_context(nc.Block())

        rows = w13[:, 0:8, :, :, :].rearrange("p e j c i -> p e (j c i)")[:, :, 0:D]

        @block.sync
        def _(sp):
            sp.dma_start(w_raw[:, :, :], w_qkv.rearrange("(r p) d -> p r d", p=P)).then_inc(wqkv_in, 16)
            for b in range(B):
                sp.dma_start(X[:, b * TB:(b + 1) * TB, :], x_tiles[:, b * TB:(b + 1) * TB, :]).then_inc(x_in[b], 16)
            sp.dma_start(bqk[:, :], b_qkv[0:2 * D].rearrange("(c p) -> p c", p=P),
                         allow_slow_non_contiguous=True).then_inc(bias_in, 16)
            sp.dma_start(bv, b_qkv[2 * D:3 * D].partition_broadcast(P)).then_inc(bias_in, 16)
            sp.dma_start(bo[:, 0, :], b_out.partition_broadcast(P)).then_inc(bias_in, 16)
            sp.dma_start(wo_raw, w_out.rearrange("(c p) d -> p c d", p=P)).then_inc(wo_in, 16)
            sp.dma_start(gate_raw, gate_w).then_inc(wo_in, 16)
            sp.dma_start(Ks[96:102, :, :, :], k_rows.rearrange("r (s g) t -> r s g t", s=4)).then_inc(rows_in, 16)
            sp.dma_start(Qs[96:99, :, :, :], k_rows[3:6].rearrange("r (s g) t -> r s g t", s=4)).then_inc(rows_in, 16)

            def load_w13(n):
                e = slice(4 * n, 4 * n + 4)
                for j, w in enumerate((w1, w3)):
                    sp.dma_start(w13[:, e, j, :, :].rearrange("p e c i -> p e (c i)"),
                                 w[e].rearrange("e (p c) i -> p e (c i)", c=KC)).then_inc(w13_in, 16)

            for n in range(3):
                load_w13(n)

            def write_pieces(r):
                _, b, m = qk_jobs[r]
                for piece, ready in enumerate((part1, part2)):
                    sp.wait_ge(ready, r + 1)
                    sp.dma_start(parts_d[b, m, piece].rearrange("d h t -> h d t"), qk_p[:, r % NQ, piece, :]
                                 ).then_inc(pieces_out[r % NQ], 16)

            def read_stack(u):
                b, g = divmod(u, 4)
                for r in (4 * b + 2 * (g // 2), 4 * b + 2 * (g // 2) + 1):
                    sp.wait_ge(pieces_out[r % NQ], 32 * (r // NQ + 1))
                    sp.wait_ge(third_out[r % NQ], 16 * (r // NQ + 1))
                if u >= 4:
                    sp.wait_ge(b_done, (u - 3) * 8)
                h0 = G * (g % 2)
                both = 1 if u >= 4 else 2
                for dst, m in ((Qs, g // 2), (Ks, 2 + g // 2)):
                    parts = parts_d[b, m, :, :, h0:h0 + both * G, :].rearrange("j d h t -> j d (h t)")
                    for first, n in ((0, 3), (3, 2), (5, 1)):
                        src = parts[0:n] if m >= 2 else parts[3 - n:4 - n].broadcast_to((n, HD, both * G * S))
                        sp.dma_start(dst[first * HD:(first + n) * HD, g:g + both, :, :].rearrange("p g h t -> p (g h t)"), src).then_inc(stack_in[g], 16)

            for r in range(len(qk_jobs)):
                write_pieces(r)
                if r in (1, 3):
                    read_stack(r - 1)
            def write_maxima(u):
                sp.wait_ge(mT_ready, u + 1)
                for j in range(3):
                    sp.dma_start(Qs[99 + j:100 + j, u % 4, :, :], mT[G * j:G * j + G, u % 2, :]).then_inc(mrow_in[u % 4], 16)

            for n in range(3, 3 + 2):
                load_w13(n)
            n += 1
            write_maxima(0)
            for u in range(UNITS - 1):
                write_maxima(u + 1)
                for k in range(8):
                    if n < E // 4 and k in (4, 6):
                        sp.wait_ge(b_done, u * 8 + k + 1)
                        load_w13(n)
                        n += 1
                if u < UNITS - 4:
                    read_stack(u + 4)
            sp.wait_ge(zero_ready, 1)
            for t in range(SURE, NT, 8):
                sp.dma_start(y_d[t * P:(t + 8) * P, :].rearrange("(t p) d -> p t d", p=P),
                             zero[:, :, :].broadcast_to((P, 8, D))).then_inc(zero_out, 16)
            sp.wait_ge(x1_ready, T)
            sp.dma_start(x1_d.rearrange("(t p) d -> p t d", p=P), X[:, :, :]).then_inc(x1_out, 16)
            sp.wait_ge(zero_out, 16 * (NT - SURE) // 8)
            for n in range(8):
                sp.dma_start(w2s[:, 8 * n:8 * n + 8, :], w2[8 * n:8 * n + 8].rearrange("e i d -> i e d")).then_inc(w2_in, 16)

            def group(g):
                for t in range(GR * g - 4, GR * g):
                    if g:
                        sp.wait_ge(yo_ready, t + 1)
                        sp.dma_start(y_d[t * P:(t + 1) * P, :], yo[:, t % 4, :]).then_inc(y_out[t % 4], 16)
                for q in y_out:
                    if g:
                        sp.wait_ge(q, 16 * g)

            expert_rounds(sp, group)
            sp.sem_inc(tiles_out, 1)
            for t in range(T):
                sp.wait_ge(fin_ready, t + 1)
                sp.dma_start(out_tiles[t], X[:, t, :]).then_inc(out_done, 16)
            sp.wait_ge(out_done, 16 * T)

        @block.gpsimd
        def _(pool):
            n = 0

            def step(ins):
                nonlocal n
                n += 1
                ins.then_inc(pool_step, 1)
                pool.wait_ge(pool_step, n)

            step(pool.memset(ident[:, :], 1.0))
            step(pool.affine_select(out=ident[:, :], in_=ident[:, :], compare_op=ALU.is_equal, fill=0.0, base=0,
                                    pattern=[[-1, P]], channel_multiplier=1))
            step(pool.memset(wo_pad, 0.0))
            pool.tensor_copy(identb[:, :], ident[:, :]).then_inc(consts, 1)
            step(pool.memset(maskA[:, :], 0.0))
            step(pool.memset(maskB[:, :], 0.0))
            pool.affine_select(out=maskA[:, :], in_=maskA[:, :], compare_op=ALU.is_ge, fill=NEG, base=0,
                               pattern=[[-1, P]], channel_multiplier=1).then_inc(consts, 1)
            pool.affine_select(out=maskB[:, :], in_=maskB[:, :], compare_op=ALU.is_ge, fill=NEG, base=0,
                               pattern=[[1, P]], channel_multiplier=-1).then_inc(consts, 1)
            pool.memset(V[:, :, :], 1.0).then_inc(consts, 1)
            pool.wait_ge(wo_in, 32)
            pool.tensor_copy(wo_pad.rearrange("p c (h d) -> p c h d", d=32)[:, :, :, 0:HD],
                             wo_raw.rearrange("p c (h d) -> p c h d", d=HD)).then_inc(pads, 1)
            for r in range(len(qk_jobs)):
                pool.wait_ge(part2, r + 1)
                pool.tensor_tensor(qk_p[:, r % NQ, 2, :], qk_r[:, r % 2, :], qk_p[:, r % NQ, 1, :],
                                   ALU.subtract).then_inc(part3, 1)
                _, b, m = qk_jobs[r]
                pool.wait_ge(part3, r + 1)
                pool.dma_start(parts_d[b, m, 2].rearrange("d h t -> h d t"), qk_p[:, r % NQ, 2, :]
                               ).then_inc(third_out[r % NQ], 16)

            pool.wait_ge(bias_in, 48)
            pool.wait_ge(pe_job, jobs.index(("xT", B - 1, KC - 1)) + 1)
            for t in range(T):
                pool.tensor_tensor(X[:, t, :], X[:, t, :], bo[:, 0, :], ALU.add).then_inc(xb_ready, 1)
            pool.wait_ge(xb_ready, T)
            pool.memset(zero[:, :, :], 0.0).then_inc(zero_ready, 1)
            step(pool.memset(upper[:, :], 1.0))
            pool.affine_select(out=upper[:, :], in_=upper[:, :], compare_op=ALU.is_gt, fill=0.0, base=0,
                               pattern=[[1, P]], channel_multiplier=-1).then_inc(consts, 1)
            pool.memset(onesb[:, :], 1.0).then_inc(consts, 1)
            pool.memset(onesf[:, :], 1.0).then_inc(consts, 1)
            pool.iota(tok_i[:, :], pattern=[[P, T]], base=0, channel_multiplier=1).then_inc(pool_step, 1)
            pool.memset(te_row[:, NT:ROUNDS].bitcast(F32), 0.0).then_inc(consts, 1)
            pool.memset(ids[:, NT:ROUNDS].bitcast(F32), 0.0).then_inc(consts, 1)
            n += 1
            pool.wait_ge(pool_step, n)
            pool.tensor_copy(tok[:, :], tok_i[:, :]).then_inc(consts, 1)
            def normalise(u):
                b, g = divmod(u, 4)
                pool.wait_ge(factor_ready, u + 1)
                pool.tensor_tensor(ctxT[:, b, g, :], OT[:, u % 2, :], factor[:, u % 2, :], ALU.mult).then_inc(ctx_ready, 1)

            for u in range(UNITS - 1):
                normalise(u)
            pool.wait_ge(x1_ready, T)
            step(pool.iota(iota_i[:, :], pattern=[[1, P], [0, 8]], base=0, channel_multiplier=0))
            pool.tensor_copy(iota_h[:, :, :].rearrange("p r k -> p (r k)"), iota_i[:, :]).then_inc(consts, 1)
            pool.wait_ge(x1_out, 16)

            pool.wait_ge(ids_ready, 1)
            def group(g):
                for i in range(GR * g, GR * g + GR):
                    if i >= NG:
                        pool.wait_ge(t_ps, i + 1 - NG)
                    pool.indirect_dma_start(gx[:, i % NG, :], None, x1_d,
                                            bass.IndirectOffsetOnAxis(ids[:, i:i + 1], 0)).then_inc(gx_in[i % NG], 16)

            expert_rounds(pool, group)
            pool.wait_ge(tiles_out, 1)
            pool.wait_ge(tiles_done, 1)
            for n in range(T * TOPK):
                t, k = divmod(n, TOPK)
                if n >= 8:
                    pool.wait_ge(rows_used, n - 7)
                pool.indirect_dma_start(rows[:, n % 8, :], None, y_d,
                                        bass.IndirectOffsetOnAxis(slot_u[:, t, k:k + 1], 0)).then_inc(row_in[n % 8], 16)

        @block.scalar
        def _(act):
            def job(i):
                kind = jobs[i][0]
                bank = ps[:, i % 8, :]
                act.wait_ge(pe_job, i + 1)
                if kind == "wT":
                    g = jobs[i][1]
                    act.copy(WT[:, :, :].rearrange("p c n -> p (c n)")[:, 512 * g:512 * g + 512], bank).then_inc(act_job, 1)
                elif kind == "woT":
                    g = jobs[i][1]
                    act.copy(WoT[:, :, :].rearrange("p g n -> p (g n)")[:, 512 * g:512 * g + 512], bank).then_inc(act_job, 1)
                else:
                    act.copy(gateT[:, :, :].rearrange("p c e -> p (c e)"), bank[:, 0:KC * E]).then_inc(act_job, 1)

            r = 0
            for i, j in enumerate(jobs):
                if j[0] in on_act:
                    job(i)
                elif j[0] == "qk":
                    if r >= NQ:
                        act.wait_ge(pieces_out[r % NQ], 32 * (r // NQ))
                        act.wait_ge(third_out[r % NQ], 16 * (r // NQ))
                    act.wait_ge(dve_job, sum(q[0] not in on_act for q in jobs[:i + 1]))
                    act.copy(qk_p[:, r % NQ, 0, :], qk_f[:, r % 2, :]).then_inc(part1, 1)
                    act.wait_ge(rest1, r + 1)
                    act.copy(qk_p[:, r % NQ, 1, :], qk_r[:, r % 2, :]).then_inc(part2, 1)
                    r += 1

            def max_rows(u):
                act.wait_ge(mT_ps, u + 1)
                if u >= 2:
                    act.wait_ge(mrow_in[(u - 2) % 4], 48 * ((u - 2) // 4 + 1))
                act.copy(mT[:, u % 2, :], ps[0:3 * G, 7, :]).then_inc(mT_ready, 1)

            def probs(u, kb, hp):
                n = u * 8 + 2 * kb + hp
                act.wait_ge(b_done, n + 1)
                if n >= PRING:
                    act.wait_ge(pv_done, n - PRING + 1)
                N = S - kb * P
                act.activation(PT[:, n % PRING, :, 0:N], slot(("B", n))[:, :, 0:N], ACT.Exp).then_inc(exp_done, 1)

            def heads_out(u):
                act.wait_ge(pv_done, 8 * (u + 1))
                if u >= 2:
                    act.wait_ge(ctx_ready, u - 1)
                act.copy(OT[:, u % 2, :], ps[:, 6, :]).then_inc(ot_ready, 1)

            def deviation(b):
                act.wait_ge(ln_var, b + 1)
                act.activation(rstd[:, b * TB:(b + 1) * TB], rstd[:, b * TB:(b + 1) * TB], ACT.Sqrt).then_inc(ln_sd, 1)

            def token_columns(t):
                act.wait_ge(r_xT_ps, pair_end(t) if t < TB else t + 1)
                if t >= 4:
                    act.wait_ge(r_log_ps, t - 3)
                act.copy(x1T[:, t % 4, :, :].rearrange("p c n -> p (c n)"), router_bank(t)[:, 0:KC * P]).then_inc(r_xT, 1)

            act.wait_ge(pe_job, len(jobs))
            act.wait_ge(part3, len(qk_jobs))
            for q in pieces_out:
                act.wait_ge(q, 32 * len(qk_jobs) // NQ)
            for q in third_out:
                act.wait_ge(q, 16 * len(qk_jobs) // NQ)
            max_rows(0)
            for u in range(UNITS):
                for kb in range(TB):
                    for hp in range(2):
                        probs(u, kb, hp)
                    if kb == 1 and u + 1 < UNITS:
                        max_rows(u + 1)
                    if kb == 0 and u >= 1:
                        heads_out(u - 1)
                    if u == UNITS - 1:
                        if kb == 0:
                            deviation(0)
                        elif kb == 2:
                            token_columns(0)
                            token_columns(1)
            heads_out(UNITS - 1)
            token_columns(2)
            token_columns(3)
            deviation(1)
            for t in range(TB, T):
                token_columns(t)
            act.wait_ge(shifted, 1)
            act.activation(Wc[:, :, :], Wc[:, :, :], ACT.Exp).then_inc(exps, 1)
            act.wait_ge(te_ps, 1)
            act.copy(te_row[:, 0:NT], ps[0:1, 6, 0:NT]).then_inc(te_out, 1)
            for t in range(T):
                act.wait_ge(ohB_ready, t + 1)
                if t >= 2:
                    act.wait_ge(oh_used, t - 1)
                act.activation(ohBt[:, t % 2, :, :].rearrange("p r k -> p (r k)"),
                               ohB[:, t % 2, :, :].rearrange("p r k -> p (r k)"), ACT.Identity, scale=tok[:, t:t + 1]
                               ).then_inc(ohBt_ready, 1)
            act.wait_ge(oh_used, T)
            act.copy(ids[:, 0:NT], ps[:, 7, 0:NT]).then_inc(ids_ready, 1)

            def round_(i):
                if i >= 1:
                    t = i - 1
                    act.wait_ge(gu_ps, t + 1)
                    act.activation(silu[:, t % 2, :], ps[:, 2 + t % 2, 0:I], ACT.Silu).then_inc(silu_ready, 1)
                if i >= 4:
                    t = i - 4
                    act.wait_ge(y_ps, t + 1)
                    if t >= 4:
                        act.wait_ge(y_out[t % 4], 16 * (t // 4))
                    act.copy(yo[:, t % 4, :], ps[:, 6 + t % 2, 0:D]).then_inc(yo_ready, 1)

            def group(g):
                for i in range(GR * g, GR * g + GR):
                    round_(i)

            expert_rounds(act, group)
            for t in range(T):
                act.wait_ge(ln_var, t + 3)
                act.activation(rstd[:, t:t + 1], rstd[:, t:t + 1], ACT.Sqrt).then_inc(ln_sd, 1)

        @block.vector
        def _(dve):
            n_step = 0

            def step(ins):
                nonlocal n_step
                n_step += 1
                ins.then_inc(dve_step, 1)
                dve.wait_ge(dve_step, n_step)

            def rest(r):
                dve.wait_ge(part1, r + 1)
                if r >= 2:
                    dve.wait_ge(part3, r - 1)
                dve.tensor_tensor(qk_r[:, r % 2, :], qk_f[:, r % 2, :], qk_p[:, r % NQ, 0, :],
                                  ALU.subtract).then_inc(rest1, 1)

            dve.wait_ge(bias_in, 48)
            r = 0
            for i, j in enumerate(jobs):
                if j[0] in on_act:
                    continue
                bank = ps[:, i % 8, :]
                dve.wait_ge(pe_job, i + 1)
                if j[0] == "xT":
                    dve.tensor_copy(xT[:, j[2], j[1] * S:(j[1] + 1) * S], bank).then_inc(dve_job, 1)
                elif j[0] == "qk":
                    b, m = j[1:]
                    if r >= 2:
                        dve.wait_ge(rest1, r - 1)
                    dve.tensor_scalar(qk_f[:, r % 2, :], bank, bqk[:, m:m + 1], 0.25 if m < 2 else 1.0,
                                      ALU.add, ALU.mult).then_inc(dve_job, 1)
                    if r >= 1:
                        rest(r - 1)
                    r += 1
                    if r == len(qk_jobs):
                        rest(r - 1)
                elif j[0] == "v":
                    for t in (2 * j[1], 2 * j[1] + 1):
                        if t == 0:
                            dve.wait_ge(consts, 4)
                        ins = dve.tensor_tensor(V[:, t, 0:H * VH].rearrange("p (h d) -> p h d", d=VH)[:, :, 0:HD],
                                                bank[:, (t % 2) * D:(t % 2) * D + D].rearrange("p (h d) -> p h d", d=HD),
                                                bv.rearrange("p (h d) -> p h d", d=HD), ALU.add)
                    ins.then_inc(dve_job, 1)

            def row_max(u, i, hp):
                n = u * 8 + 2 * i + hp
                dve.wait_ge(a_done, n + 1)
                if i == 0 and hp == 0 and u >= 2:
                    dve.wait_ge(mT_ps, u - 1)
                dve.tensor_reduce(mx[:, u % 2, i, 2 * hp:2 * hp + 2], slot(("A", n))[:, :, 0:(i + 1) * P],
                                  AX.X, ALU.max).then_inc(max_done, 1)

            def max_parts(u):
                m, rr, m3 = mx[:, u % 2], mr[:, u % 2], mx3[:, u % 2]
                dve.wait_ge(max_done, 8 * (u + 1))
                step(dve.tensor_scalar(m3[:, :, 0, :], m, -1.0, None, ALU.mult))
                step(dve.scalar_tensor_tensor(out=rr, in0=m, scalar=-1.0, in1=m3[:, :, 0, :], op0=ALU.mult, op1=ALU.subtract))
                step(dve.tensor_copy(m3[:, :, 1, :], rr))
                dve.tensor_tensor(m3[:, :, 2, :], rr, m3[:, :, 1, :], ALU.subtract).then_inc(mx3_ready, 1)

            def invert(u):
                dve.wait_ge(ot_ready, u + 1)
                step(dve.transpose(OB[:, :], OT[:, u % 2, :]))
                step(dve.reciprocal(rsum[:, :], OB[:, :].rearrange("p (n r) -> p n r", r=32)[:, :, HD]))
                if u >= 2:
                    dve.wait_ge(ctx_ready, u - 1)
                dve.transpose(factor[:, u % 2, :].rearrange("p (n r) -> p n r", r=32),
                              rsum[:, :].unsqueeze(2).broadcast_to((P, S // 32, 32))).then_inc(factor_ready, 1)

            def residual(t):
                dve.wait_ge(proj_ps, pair_end(t))
                dve.wait_ge(xb_ready, t + 1)
                dve.tensor_tensor(X[:, t, :], proj_bank(t), X[:, t, :], ALU.add).then_inc(y_ready, 1)
                dve.wait_ge(y_ready, t + 1)
                step(dve.bn_stats(stats[:, t, :], X[:, t, :]))

            def variance(b):
                for t in range(b * TB, (b + 1) * TB):
                    ins = dve.bn_aggr(mv[:, t, :], stats[:, t, :])
                step(ins)
                dve.tensor_scalar(rstd[:, b * TB:(b + 1) * TB], mv[:, b * TB:(b + 1) * TB, 1], EPS, None, ALU.add).then_inc(ln_var, 1)

            def first_norm(b):
                dve.wait_ge(ln_sd, b + 1)
                step(dve.reciprocal(rstd[:, b * TB:(b + 1) * TB], rstd[:, b * TB:(b + 1) * TB]))
                for t in range(b * TB, (b + 1) * TB):
                    dve.tensor_scalar(X[:, t, :], X[:, t, :], mv[:, t, 0:1], rstd[:, t:t + 1],
                                      ALU.subtract, ALU.mult).then_inc(x1_ready, 1)

            def route(t):
                dve.wait_ge(r_log_ps, pair_end(t) if t < TB else t + 1)
                step(dve.tensor_copy(L[:, t, :], router_bank(t)[:, 0:E]))
                step(dve.max(top8[:, t, :], L[:, t, :]))
                step(dve.match_replace(out=Sl[:, t, :], in_to_replace=top8[:, t, :], in_values=L[:, t, :],
                                       imm_value=-3.0e38))
                dve.tensor_tensor(Mk[:, t, :], Sl[:, t, :], L[:, t, :], ALU.not_equal).then_inc(mask_ready, 1)

            for u in range(2):
                for i in range(TB):
                    row_max(u, i, 0)
                    row_max(u, i, 1)
                max_parts(u)
            for u in range(UNITS):
                for i in range(TB):
                    if i == 2 and u >= 1:
                        invert(u - 1)
                    if u + 2 < UNITS:
                        row_max(u + 2, i, 0)
                    if u == UNITS - 2 and i == 1:
                        residual(0)
                        residual(1)
                    if u + 2 < UNITS:
                        row_max(u + 2, i, 1)
                    if u == UNITS - 2 and i == 3:
                        residual(2)
                        residual(3)
                if u + 2 < UNITS:
                    max_parts(u + 2)
                if u == UNITS - 2:
                    variance(0)
                    first_norm(0)
            route(0)
            route(1)
            invert(UNITS - 1)
            dve.wait_ge(factor_ready, UNITS)
            dve.tensor_tensor(ctxT[:, 1, 3, :], OT[:, 1, :], factor[:, 1, :], ALU.mult).then_inc(last_ctx, 1)
            route(2)
            route(3)
            for t in range(TB, T):
                residual(t)
            variance(1)
            first_norm(1)
            for t in range(TB, T):
                route(t)
            dve.tensor_tensor(Wc[:, :, :], L[:, :, :], top8[:, :, 0:1].broadcast_to((P, T, E)), ALU.subtract).then_inc(shifted, 1)
            dve.wait_ge(pos_ps, T)
            step(dve.tensor_scalar(cnt_i[:, 0, :], ps[:, 1, 0:E], float(P - 1), None, ALU.add))
            step(dve.tensor_scalar(cnt_i[:, 1, :], cnt_i[:, 0, :], 7, None, ALU.logical_shift_right))
            step(dve.tensor_copy(cnt[:, 0, :], cnt_i[:, 1, :]))
            dve.wait_ge(consts, 11)
            step(dve.tensor_tensor_scan(cnt[:, 1, :], onesf[:, :], cnt[:, 0, :], 0.0, ALU.mult, ALU.add))
            dve.tensor_copy(used_i[:, :], cnt[0:1, 1, E - 1:E]).then_inc(used_ready, 1)
            step(dve.tensor_tensor(cnt[:, 2, :], cnt[:, 1, :], cnt[:, 0, :], ALU.subtract))
            step(dve.tensor_scalar(cnt[:, 3, :], cnt[:, 2, :], float(P), 1.0, ALU.mult, ALU.add))
            step(dve.tensor_scalar(te[:, 0:E], cnt[:, 1, :], tok[:, 0:1], None, ALU.is_le))
            step(dve.tensor_reduce(te[:, E:E + 1], te[:, 0:E], AX.X, ALU.add))
            dve.tensor_scalar(te[:, 0:1], te[:, E:E + 1], float(E - 1), None, ALU.min).then_inc(te_ready, 1)
            step(dve.tensor_tensor(Sl[:, :, :], ps[:, 0, :].rearrange("p (t e) -> p t e", e=E),
                                   cnt[:, 3:4, :].broadcast_to((P, T, E)), ALU.add))
            step(dve.tensor_tensor(Sl[:, :, :], Sl[:, :, :], Mk[:, :, :], ALU.mult))
            for t in range(T):
                ins = dve.max(sl8[:, t, :], Sl[:, t, :])
            step(ins)
            step(dve.tensor_scalar(slot_i[:, :, :], sl8[:, :, :], -1.0, None, ALU.add))
            dve.tensor_copy(slot_u[:, :, :], slot_i[:, :, :])
            dve.tensor_scalar(part_i[:, 0], slot_i[:, :, :], P - 1, None, ALU.bitwise_and)
            step(dve.tensor_scalar(part_i[:, 1], slot_i[:, :, :], 7, None, ALU.logical_shift_right))
            step(dve.tensor_copy(part_h[:, :, :, :], part_i[:, :, :, :]))
            for t in range(T):
                if t >= 2:
                    dve.wait_ge(ohBt_ready, t - 1)
                dve.tensor_tensor(ohB[:, t % 2, :, :], iota_h[:, :, :], part_h[:, 1, t:t + 1, :].broadcast_to((P, P, 8)),
                                  ALU.is_equal).then_inc(ohB_ready, 1)
                if t >= 2:
                    dve.wait_ge(oh_used, t - 1)
                dve.tensor_tensor(ohA[:, t % 2, :, :], iota_h[:, :, :], part_h[:, 0, t:t + 1, :].broadcast_to((P, P, 8)),
                                  ALU.is_equal).then_inc(ohA_ready, 1)
            dve.wait_ge(exps, 1)
            step(dve.tensor_reduce(zs[:, 0, :], Wc[:, :, :], AX.X, ALU.add))
            step(dve.tensor_tensor(Wc[:, :, :], Wc[:, :, :], Mk[:, :, :], ALU.mult))
            step(dve.tensor_reduce(zs[:, 1, :], Wc[:, :, :], AX.X, ALU.add))
            step(dve.scalar_tensor_tensor(out=zs[:, 2, :], in0=zs[:, 0, :], scalar=1e-20, in1=zs[:, 1, :],
                                          op0=ALU.mult, op1=ALU.add))
            step(dve.reciprocal(zs[:, 3, :], zs[:, 2, :]))
            for t in range(T):
                ins = dve.tensor_scalar(Wc[:, t, :], Wc[:, t, :], zs[:, 3, t:t + 1], None, ALU.mult)
            step(ins)

            def round_(i):
                dve.wait_ge(t_ps, i + 1)
                dve.tensor_copy(gxT[:, i % 2, :, :].rearrange("p c n -> p (c n)"), ps[:, i % 2, 0:KC * P]).then_inc(gxT_ready, 1)
                if i >= 3:
                    t = i - 3
                    dve.wait_ge(aT_ps, t + 1)
                    if t >= 2:
                        dve.wait_ge(y_ps, t - 1)
                    dve.tensor_copy(aT[:, t % 2, :], ps[0:I, 4 + t % 2, 0:P]).then_inc(aT_ready, 1)
                if i >= 1:
                    t = i - 1
                    dve.wait_ge(silu_ready, t + 1)
                    dve.tensor_tensor(act_a[:, t % 2, :], silu[:, t % 2, :], ps[:, 2 + t % 2, I:2 * I],
                                      ALU.mult).then_inc(a_ready, 1)
                if i < T * TOPK:
                    t, k = divmod(i, TOPK)
                    if i >= 4:
                        dve.wait_ge(wk_ready, i - 3)
                    dve.scalar_tensor_tensor(out=junk[:, i % 4, :], in0=Sl[:, t, :], scalar=sl8[:, t, k:k + 1],
                                             in1=Wc[:, t, :], op0=ALU.is_equal, op1=ALU.mult,
                                             accum_out=wk[:, t, k:k + 1]).then_inc(wk_ready, 1)

            def group(g):
                for i in range(GR * g, GR * g + GR):
                    round_(i)

            expert_rounds(dve, group)

            dve.wait_ge(wk_ready, T * TOPK)
            for t in range(T):
                for k in range(TOPK):
                    n = t * TOPK + k
                    dve.wait_ge(row_in[n % 8], 16 * (n // 8 + 1))
                    if n:
                        dve.wait_ge(rows_used, n)
                    dve.scalar_tensor_tensor(out=X[:, t, :], in0=rows[:, n % 8, :], scalar=wk[:, t, k:k + 1], in1=X[:, t, :],
                                             op0=ALU.mult, op1=ALU.add).then_inc(rows_used, 1)
                dve.wait_ge(rows_used, (t + 1) * TOPK)
                step(dve.bn_stats(stats[:, t, :], X[:, t, :]))
                step(dve.bn_aggr(mv[:, t, :], stats[:, t, :]))
                dve.tensor_scalar(rstd[:, t:t + 1], mv[:, t, 1:2], EPS, None, ALU.add).then_inc(ln_var, 1)
                dve.wait_ge(ln_sd, t + 3)
                step(dve.reciprocal(rstd[:, t:t + 1], rstd[:, t:t + 1]))
                dve.tensor_scalar(X[:, t, :], X[:, t, :], mv[:, t, 0:1], rstd[:, t:t + 1],
                                  ALU.subtract, ALU.mult).then_inc(fin_ready, 1)

        @block.tensor
        def _(pe):
            pe.wait_ge(consts, 1)
            pe.wait_ge(wqkv_in, 16)
            for i, j in enumerate(jobs):
                kind, bank = j[0], ps[:, i % 8, :]
                if i >= 8:
                    evacuated(pe, i - 8)
                if kind == "wT":
                    for n in range(4):
                        c, r = divmod(4 * j[1] + n, 6)
                        last = pe.transpose(bank[:, n * P:(n + 1) * P], w_raw[:, r, c * P:(c + 1) * P], ident[:, :])
                elif kind == "xT":
                    b, c = j[1:]
                    pe.wait_ge(x_in[b], 16)
                    for t in range(TB):
                        last = pe.transpose(bank[:, t * P:(t + 1) * P], X[:, b * TB + t, c * P:(c + 1) * P], ident[:, :])
                elif kind == "qk":
                    b, m = j[1:]
                    if m == 0:
                        evacuated(pe, 2)
                        evacuated(pe, jobs.index(("xT", b, KC - 1)))
                    for c in range(KC):
                        last = pe.matmul(bank, WT[:, c, m * P:(m + 1) * P], xT[:, c, b * S:(b + 1) * S],
                                         start=(c == 0), stop=(c == KC - 1))
                elif kind == "v":
                    for t in (2 * j[1], 2 * j[1] + 1):
                        for c in range(KC):
                            last = pe.matmul(bank[:, (t % 2) * D:(t % 2) * D + D], xT[:, c, t * P:(t + 1) * P],
                                             WT[:, c, 2 * D:3 * D], start=(c == 0), stop=(c == KC - 1))
                elif kind == "woT":
                    pe.wait_ge(pads, 1)
                    for n in range(4):
                        g, c = divmod(4 * j[1] + n, KC)
                        last = pe.transpose(bank[:, n * P:(n + 1) * P], wo_pad[:, c, g * P:(g + 1) * P], ident[:, :])
                else:
                    for c in range(KC):
                        last = pe.transpose(bank[:, c * E:(c + 1) * E], gate_raw[:, c * P:(c + 1) * P], ident[0:E, 0:E])
                last.then_inc(pe_job, 1)
            def bank_left(bank):
                evacuated(pe, max(i for i in range(len(jobs)) if i % 8 == bank))

            pe.wait_ge(consts, 4)
            pe.wait_ge(rows_in, 32)

            def scores_A(u, i, hp):
                s = u % 4
                if i == 0 and hp == 0:
                    if u < 4:
                        pe.wait_ge(stack_in[s - s % 2], 96)
                    else:
                        pe.wait_ge(stack_in[s], 96 * (2 - s % 2))
                n = u * 8 + 2 * i + hp
                if n < SLOTS:
                    bank_left(2 * n)
                    bank_left(2 * n + 1)
                slot_free(pe, ("A", n))
                dst = slot(("A", n))
                for j in range(2):
                    h = 2 * hp + j
                    pe.matmul(dst[:, j, 0:(i + 1) * P], Qs[0:99, s, h, i * P:(i + 1) * P], Ks[0:99, s, h, 0:(i + 1) * P],
                              start=True, stop=False)
                    last = pe.matmul(dst[:, j, i * P:(i + 1) * P], identb[:, :], maskA[:, :], start=False, stop=True)
                last.then_inc(a_done, 1)

            def scores_B(u, kb, hp):
                s = u % 4
                if kb == 0 and hp == 0:
                    pe.wait_ge(mrow_in[s], 48 * (u // 4 + 1))
                n = u * 8 + 2 * kb + hp
                slot_free(pe, ("B", n))
                dst = slot(("B", n))
                for j in range(2):
                    h = 2 * hp + j
                    pe.matmul(dst[:, j, 0:S - kb * P], Ks[:, s, h, kb * P:(kb + 1) * P], Qs[:, s, h, kb * P:S],
                              start=True, stop=False)
                    last = pe.matmul(dst[:, j, 0:P], identb[:, :], maskB[:, :], start=False, stop=True)
                last.then_inc(b_done, 1)

            def values(u, kb):
                b, g = divmod(u, 4)
                if kb == 0 and u:
                    pe.wait_ge(ot_ready, u)
                elif kb == 0:
                    bank_left(6)
                for hp in range(2):
                    n = u * 8 + 2 * kb + hp
                    pe.wait_ge(exp_done, n + 1)
                    for j in range(2):
                        h = 2 * hp + j
                        last = pe.matmul(ps[32 * h:32 * h + 32, 6, kb * P:S],
                                         V[:, b * TB + kb, (G * g + h) * VH:(G * g + h) * VH + 32],
                                         PT[:, n % PRING, j, 0:S - kb * P], start=(kb == 0), stop=(kb == TB - 1))
                    last.then_inc(pv_done, 1)

            def max_rows(u):
                pe.wait_ge(mx3_ready, u + 1)
                if u:
                    pe.wait_ge(mT_ready, u)
                else:
                    bank_left(7)
                for i in range(TB):
                    last = pe.matmul(ps[0:3 * G, 7, i * P:(i + 1) * P],
                                     mx3[:, u % 2, i, :, :].rearrange("p j h -> p (j h)"), identb[:, :], start=True, stop=True)
                last.then_inc(mT_ps, 1)

            def project(t):
                if t % 2 == 0:
                    pe.wait_ge(ctx_ready, 4)
                    pe.wait_ge(mT_ready, UNITS)
                    if t:
                        pe.wait_ge(y_ready, t)
                for g in range(4):
                    last = pe.matmul(proj_bank(t), ctxT[:, 0, g, t * P:(t + 1) * P], WoT[:, g, :],
                                     start=(g == 0), stop=(g == 3))
                last.then_inc(proj_ps, 1)

            def project_unit(g):
                if g < 3:
                    pe.wait_ge(ctx_ready, TB + g + 1)
                else:
                    pe.wait_ge(last_ctx, 1)
                if g == 0:
                    slot_read(pe, [v for v in uses if slot_of[v] == 2][-1])
                for t in range(TB, T):
                    last = pe.matmul(proj_bank(t), ctxT[:, 1, g, (t - TB) * P:(t - TB + 1) * P], WoT[:, g, :],
                                     start=(g == 0 and t % 2 == 0), stop=(g == 3 and t % 2 == 1))
                    if g == 3:
                        last.then_inc(proj_ps, 1)

            def turn(t):
                pe.wait_ge(x1_ready, t + 1)
                if t >= 2:
                    pe.wait_ge(mask_ready, min(t - t % 2, TB))
                for c in range(KC):
                    last = pe.transpose(router_bank(t)[:, c * P:(c + 1) * P], X[:, t, c * P:(c + 1) * P], ident[:, :])
                last.then_inc(r_xT_ps, 1)

            def logits(t):
                pe.wait_ge(r_xT, pair_end(t) if t < TB else t + 1)
                for c in range(KC):
                    last = pe.matmul(router_bank(t)[:, 0:E], x1T[:, t % 4, c, :], gateT[:, c, :], start=(c == 0), stop=(c == KC - 1))
                last.then_inc(r_log_ps, 1)

            def places(q):
                if q == 0:
                    pe.wait_ge(consts, 6)
                pe.wait_ge(mask_ready, q + 1)
                pe.matmul(ps[:, 0, q * E:(q + 1) * E], upper[:, :], Mk[:, q, :], start=(q == 0), stop=(q == T - 1))
                if q < T - 1:
                    pe.matmul(ps[:, 0, (q + 1) * E:T * E].rearrange("p (t e) -> p t e", e=E), onesb[:, :],
                              Mk[:, q:q + 1, :].broadcast_to((P, T - 1 - q, E)), start=False, stop=False)
                pe.matmul(ps[:, 1, 0:E], onesb[:, :], Mk[:, q, :], start=(q == 0), stop=(q == T - 1)).then_inc(pos_ps, 1)

            for i in range(TB):
                for hp in range(2):
                    scores_A(0, i, hp)
            for i in range(TB):
                if i == 1:
                    max_rows(0)
                for hp in range(2):
                    scores_A(1, i, hp)
            for u in range(UNITS):
                for i in range(TB):
                    for hp in range(2):
                        scores_B(u, i, hp)
                        if u + 2 < UNITS:
                            scores_A(u + 2, i, hp)
                    if i == 1 and u + 1 < UNITS:
                        max_rows(u + 1)
                    if i:
                        values(u, i - 1)
                    elif u:
                        values(u - 1, TB - 1)
                    if u == UNITS - 2 and i % 2 == 1:
                        project(i - 1)
                        project(i)
                    if u == UNITS - 1:
                        if i == 0:
                            project_unit(0)
                        if i == 1:
                            project_unit(1)
                        if i == 1:
                            turn(0)
                            turn(1)
                        elif i == 2:
                            logits(0)
                            logits(1)
            values(UNITS - 1, TB - 1)
            turn(2)
            turn(3)
            project_unit(2)
            logits(2)
            logits(3)
            project_unit(3)
            for t in range(TB, T):
                turn(t)
            for t in range(TB, T):
                logits(t)
            for t in range(T):
                places(t)
            pe.wait_ge(te_ready, 1)
            pe.matmul(ps[0:1, 6, 0:NT], te[:, 0:1], ident[:, :], start=True, stop=True).then_inc(te_ps, 1)
            for t in range(T):
                pe.wait_ge(ohA_ready, t + 1)
                pe.wait_ge(ohBt_ready, t + 1)
                for k in range(TOPK):
                    last = pe.matmul(ps[:, 7, 0:NT], ohA[:, t % 2, :, k], ohBt[:, t % 2, :, k], start=(t == 0 and k == 0),
                                     stop=(t == T - 1 and k == TOPK - 1))
                last.then_inc(oh_used, 1)
            pe.wait_ge(te_out, 1)
            pe.wait_ge(w13_in, 16 * 2 * E // 4)

            e = {}

            def round_(i):
                pe.wait_ge(gx_in[i % NG], 16 * (i // NG + 1))
                v = gx[:, i % NG, :].rearrange("p (n c) -> p c n", c=KC)
                for c in range(KC):
                    last = pe.transpose(ps[:, i % 2, c * P:(c + 1) * P], v[:, c, :], ident[:, :])
                last.then_inc(t_ps, 1)
                e[i] = pe.value_load(te_row[0:1, i:i + 1], min_val=0, max_val=E - 1)
                if i >= 3:
                    t = i - 3
                    pe.wait_ge(a_ready, t + 1)
                    pe.transpose(ps[0:I, 4 + t % 2, 0:P], act_a[:, t % 2, :], ident[:, :]).then_inc(aT_ps, 1)
                if i >= 1:
                    t = i - 1
                    pe.wait_ge(gxT_ready, t + 1)
                    for c in range(KC):
                        last = pe.matmul(ps[:, 2 + t % 2, 0:2 * I], gxT[:, t % 2, c, :],
                                         w13[:, bass.ds(e[t], 1), :, c, :].rearrange("p a j i -> p (a j) i"),
                                         start=(c == 0), stop=(c == KC - 1))
                    last.then_inc(gu_ps, 1)
                if i >= 4:
                    t = i - 4
                    pe.wait_ge(aT_ready, t + 1)
                    if t >= 2:
                        pe.wait_ge(yo_ready, t - 1)
                    else:
                        pe.wait_ge(w2_in, 16 * 8)
                    pe.matmul(ps[:, 6 + t % 2, 0:D], aT[:, t % 2, :], w2s[:, bass.ds(e.pop(t), 1), :].rearrange("p a d -> p (a d)"),
                              start=True, stop=True).then_inc(y_ps, 1)

            def group(g):
                for i in range(GR * g, GR * g + GR):
                    round_(i)

            expert_rounds(pe, group)
            pe.drain().then_inc(tiles_done, 1)


_INS = ['L0_attn_x', 'L0_attn_Wqkv', 'L0_attn_b_qkv', 'L0_attn_Wout', 'L0_attn_b_out', 'L0_ffn_gate_w', 'L0_ffn_w1',
        'L0_ffn_w3', 'L0_ffn_w2']
_OUTS = [((2, 512, 256), 'float32')]


def kernel(**inputs):
    import numpy as _np
    import concourse.bacc as _bacc
    from concourse import mybir as _mybir
    from concourse.bass_utils import run_bass_kernel_spmd as _run

    nc = _bacc.Bacc("TRN2", target_bir_lowering=False, num_devices=1)
    arrays, args = {}, []
    for name in _INS:
        a = _np.ascontiguousarray(inputs[name])
        arrays[f"in_{name}_dram"] = a
        args.append(nc.dram_tensor(f"in_{name}_dram", a.shape, _mybir.dt.from_np(a.dtype), kind="ExternalInput").ap())
    for i, (shape, dtype) in enumerate(_OUTS):
        dt = _mybir.dt.from_np(_np.dtype(dtype))
        args.append(nc.dram_tensor(f"out_{i}_dram", shape, dt, kind="ExternalOutput").ap())
    layer(nc, *args)
    r = _run(nc, [arrays], core_ids=[0])
    got = tuple(r.results[0][f"out_{i}_dram"] for i in range(len(_OUTS)))
    return got[0]
```
